# Optimizing a Trainium2 kernel written in Bass

```python
import numpy as np
import jax
import jax.numpy as jnp

def _softmax(x, axis=-1):
    return jax.nn.softmax(x, axis=axis)

def _gelu(x):
    return jax.nn.gelu(x, approximate=True)

def _silu(x):
    return jax.nn.silu(x)

def _sigmoid(x):
    return jax.nn.sigmoid(x)

def _layernorm(x, axis=-1, eps=1e-05):
    m = jnp.mean(x, axis=axis, keepdims=True)
    v = jnp.var(x, axis=axis, keepdims=True)
    return (x - m) / jnp.sqrt(v + eps)

def _scatter_add(tgt, idx, src, axis=0):
    return tgt.at[idx].add(src)

def _segment_sum(src, seg, n):
    return jax.ops.segment_sum(src, seg, n)
kernel_name = 'mk_adj_preln_d1_adj_r2_63244f'

def setup_inputs(seed: int=0):
    np.random.seed(seed)
    _w = jnp.asarray

    def _rec_inputs():
        import jax
        import jax.numpy as jnp
        _gk = jax.random.key(seed)
        x = -0.0005963 + 1.001 * jax.random.normal(jax.random.fold_in(_gk, 1), (4096, 256), jnp.float32)
        _w = (1.0 + jnp.arange(4096, dtype=jnp.float32)) ** (-0.5)
        _w = _w / _w.mean()
        _pij = jnp.clip(0.00195312 * _w[:, None] * _w[None, :], 0.0, 1.0)
        _a = jax.random.uniform(jax.random.fold_in(_gk, 2), (4096, 4096)) < _pij
        _af = _a.astype(jnp.float32)
        adj = _af
        return (x, adj)
    x, adj = _rec_inputs()

    def _L0_gnn_setup():
        import jax, jax.numpy as jnp
        import numpy as np
        N = 3072
        D_IN = 256
        D_OUT = 256
        DENSITY = 0.005
        key = jax.random.key(seed)
        ks = jax.random.split(key, 12)
        x = jax.random.normal(ks[0], (N, D_IN), dtype=jnp.float32)
        adj_a = (jax.random.uniform(ks[1], (N, N)) < DENSITY).astype(jnp.float32)
        adj_b = (jax.random.uniform(ks[2], (N, N)) < DENSITY).astype(jnp.float32)
        W_sa = jax.random.normal(ks[3], (D_IN, D_OUT), dtype=jnp.float32) * (1.414 / np.sqrt(D_IN + D_OUT))
        a_sa = jax.random.normal(ks[4], (1, 2 * D_OUT), dtype=jnp.float32) * (1.414 / np.sqrt(1 + 2 * D_OUT))
        stdv = 1.0 / np.sqrt(D_OUT)
        W_gcnb = jax.random.uniform(ks[5], (D_IN, D_OUT), minval=-stdv, maxval=stdv, dtype=jnp.float32)
        b_gcnb = jax.random.uniform(ks[6], (D_OUT,), minval=-stdv, maxval=stdv, dtype=jnp.float32)
        s = 1.0 / np.sqrt(2 * D_IN)
        Wa = jax.random.uniform(ks[7], (1, 2 * D_IN), minval=-s, maxval=s, dtype=jnp.float32)
        ba = jax.random.uniform(ks[8], (1,), minval=-s, maxval=s, dtype=jnp.float32)
        Wb = jax.random.uniform(ks[9], (1, 2 * D_IN), minval=-s, maxval=s, dtype=jnp.float32)
        bb = jax.random.uniform(ks[10], (1,), minval=-s, maxval=s, dtype=jnp.float32)
        return {'x': x, 'adj_a': adj_a, 'adj_b': adj_b, 'W_sa': W_sa, 'a_sa': a_sa, 'W_gcnb': W_gcnb, 'b_gcnb': b_gcnb, 'Wa': Wa, 'ba': ba, 'Wb': Wb, 'bb': bb}
    _L0_gnn_all = _L0_gnn_setup()
    _L0_gnn_in = {k: v for k, v in _L0_gnn_all.items() if k in ('W_sa', 'a_sa', 'W_gcnb', 'b_gcnb', 'Wa', 'ba', 'Wb', 'bb')}
    del _L0_gnn_all
    return {'x': x, 'adj': adj, 'L0_gnn_W_sa': _L0_gnn_in['W_sa'], 'L0_gnn_a_sa': _L0_gnn_in['a_sa'], 'L0_gnn_W_gcnb': _L0_gnn_in['W_gcnb'], 'L0_gnn_b_gcnb': _L0_gnn_in['b_gcnb'], 'L0_gnn_Wa': _L0_gnn_in['Wa'], 'L0_gnn_ba': _L0_gnn_in['ba'], 'L0_gnn_Wb': _L0_gnn_in['Wb'], 'L0_gnn_bb': _L0_gnn_in['bb']}

def reference(x, adj, L0_gnn_W_sa, L0_gnn_a_sa, L0_gnn_W_gcnb, L0_gnn_b_gcnb, L0_gnn_Wa, L0_gnn_ba, L0_gnn_Wb, L0_gnn_bb):
    import jax
    import jax.numpy as jnp

    def _L0_gnn_ref(x, adj_a, adj_b, W_sa, a_sa, W_gcnb, b_gcnb, Wa, ba, Wb, bb):
        import jax, jax.numpy as jnp
        import numpy as np
        N = 3072
        D_IN = 256
        D_OUT = 256
        DENSITY = 0.005
        type_sum_a = adj_a @ x
        type_sum_b = adj_b @ x
        attn_a = jax.nn.sigmoid(jnp.concatenate([type_sum_a, x], axis=1) @ Wa.T + ba)
        attn_b = jax.nn.sigmoid(jnp.concatenate([type_sum_b, x], axis=1) @ Wb.T + bb)
        h = x @ W_sa
        Hd = h.shape[1]
        s_left = h @ a_sa[0, :Hd]
        s_right = h @ a_sa[0, Hd:]
        scores = s_left[:, None] + s_right[None, :]
        e = jnp.where(adj_a != 0, jnp.exp(-jax.nn.leaky_relu(scores, 0.01)), 0.0)
        attn = e / (jnp.sum(e, axis=1, keepdims=True) + 1e-05)
        x_a = attn @ h
        x_b = adj_b @ (x @ W_gcnb) + b_gcnb
        return jax.nn.sigmoid(attn_a * x_a + attn_b * x_b)
    h = jnp.maximum(_layernorm(x, axis=-1), 0.0)
    x = x + _L0_gnn_ref(h, adj, adj, L0_gnn_W_sa, L0_gnn_a_sa, L0_gnn_W_gcnb, L0_gnn_b_gcnb, L0_gnn_Wa, L0_gnn_ba, L0_gnn_Wb, L0_gnn_bb)
    return x

_drawn_inputs = setup_inputs


def setup_inputs(seed=0):
    import zlib

    import numpy as np

    out = dict(_drawn_inputs(seed))
    spreads = {}
    factors = {'L0_gnn_a_sa': 8.0, 'L0_gnn_b_gcnb': 8.0, 'L0_gnn_Wa': 4.358}
    for name, (base, spread) in spreads.items():
        noise = np.random.default_rng([zlib.crc32(name.encode()), seed]).standard_normal(out[name].shape)
        drawn = base * np.exp(spread * noise) if base else spread * noise
        out[name] = jnp.asarray(drawn.astype(out[name].dtype))
    for name, factor in factors.items():
        out[name] = (out[name] * factor).astype(out[name].dtype)
    return out
```

```python
from contextlib import ExitStack

import numpy as np

import concourse.bass as bass
from concourse import mybir

F32 = mybir.dt.float32
F32R = mybir.dt.float32r
ALU = mybir.AluOpType
ACT = mybir.ActivationFunctionType
AX_X = mybir.AxisListType.X

P = 128
GB = 4
GW = GB * P
SLOPE = 0.01
LN_EPS = 1e-5
DEN_EPS = 1e-5
Z_MIN = -88.0
RING = 4


def build(nc, x, adjt, w_sa, a_sa, w_gcn, b_gcn, w_a, b_a, w_b, b_b, out):
    N, D = x.shape
    NB = N // P
    NG = N // GW
    KC = D // P
    WC = D + 4
    MC = D + 2
    LEAD = 7
    PLEAD = 12
    assert NB % RING == 0 and NB > 2 * PLEAD - RING and D == 2 * P

    sl_dram = nc.dram_tensor("sl_scratch", [NB, P], F32, kind="Internal").ap()

    with ExitStack() as top:
        def sem(name):
            return top.enter_context(nc.semaphore(name))

        def sbuf(stack, name, shape, dt):
            return stack.enter_context(nc.sbuf_tensor(name, shape, dt))

        def psum(stack, name, shape, dt):
            return stack.enter_context(nc.psum_tensor(name, shape, dt))

        feat_hi = sbuf(top, "feat_hi", [P, NB, 2, WC], F32R)
        feat_lo = sbuf(top, "feat_lo", [P, NB, 2, WC], F32R)
        raw = sbuf(top, "raw", [P, RING, GW], F32)
        mask = sbuf(top, "mask", [P, RING, GW], F32R)
        node = sbuf(top, "node", [P, NB, 4], F32)
        neg_r = sbuf(top, "neg_r", [P, NB], F32)
        cap = sbuf(top, "cap", [P, NB], F32)
        cfac = sbuf(top, "cfac", [P, NB], F32)
        bias_bc = sbuf(top, "bias_bc", [P, D], F32)
        gate_b = sbuf(top, "gate_b", [P, 2], F32)

        pa = ExitStack()
        xin = sbuf(pa, "xin", [P, 4, D], F32)
        xn = sbuf(pa, "xn", [P, 2, D], F32)
        xt_hi = sbuf(pa, "xt_hi", [P, 2, KC, P], F32R)
        xt_lo = sbuf(pa, "xt_lo", [P, 2, KC, P], F32R)
        wraw = sbuf(pa, "wraw", [P, KC, 2, WC], F32)
        w_hi = sbuf(pa, "w_hi", [P, KC, 2, WC], F32R)
        w_lo = sbuf(pa, "w_lo", [P, KC, 2, WC], F32R)
        a_bc = sbuf(pa, "a_bc", [P, 2, D], F32)
        wprod = sbuf(pa, "wprod", [P, KC, 2, D], F32)
        ident = sbuf(pa, "ident", [P, P], F32)
        stats = sbuf(pa, "stats", [P, 4, 6], F32)
        mv = sbuf(pa, "mv", [P, 4, 2], F32)
        half = sbuf(pa, "half", [P, 1], F32)
        veps = sbuf(pa, "veps", [P, 4], F32)
        rstd = sbuf(pa, "rstd", [P, 4], F32)
        mr = sbuf(pa, "mr", [P, 4], F32)
        nmr = sbuf(pa, "nmr", [P, 4], F32)
        lcol = sbuf(pa, "lcol", [P, NB], F32)
        lrow = sbuf(pa, "lrow", [NB, P], F32)
        pt = psum(pa, "pt", [P, 2, 512], F32)
        pf = psum(pa, "pf", [P, 2, 2, 512], F32)
        pl = psum(pa, "pl", [P, 512], F32)
        pa.close()

        lbc = sbuf(top, "lbc", [P, NG, GW], F32)
        e = sbuf(top, "e", [P, RING, GW], F32)
        g_hi = sbuf(top, "g_hi", [P, RING, GW], F32R)
        g_lo = sbuf(top, "g_lo", [P, RING, GW], F32R)
        stage = sbuf(top, "stage", [P, GB, 2, WC], F32)
        xres = sbuf(top, "xres", [P, GB, D], F32)
        z = sbuf(top, "z", [P, GB, 2], F32)
        zc = sbuf(top, "zc", [P, GB, 2], F32)
        ez = sbuf(top, "ez", [P, GB, 2], F32)
        ez1 = sbuf(top, "ez1", [P, GB, 2], F32)
        gate = sbuf(top, "gate", [P, GB, 2], F32)
        dn = sbuf(top, "dn", [P, GB], F32)
        dn1 = sbuf(top, "dn1", [P, GB], F32)
        rdn = sbuf(top, "rdn", [P, GB], F32)
        crdn = sbuf(top, "crdn", [P, GB], F32)
        ca = sbuf(top, "ca", [P, GB], F32)
        acc = psum(top, "acc", [P, GB, 2, 512], F32)

        w_in = sem("w_in")
        x_in = [sem("x_in0"), sem("x_in1")]
        const_done = sem("const_done")
        w_zero = sem("w_zero")
        w_step = sem("w_step")
        w_ready = sem("w_ready")
        stat_done = sem("stat_done")
        mv_done = sem("mv_done")
        pow_step = sem("pow_step")
        xn_done = sem("xn_done")
        xt_done = sem("xt_done")
        xhi_done = sem("xhi_done")
        xlo_done = sem("xlo_done")
        feat_done = sem("feat_done")
        fhi_done = sem("fhi_done")
        flo_done = sem("flo_done")
        node_step = sem("node_step")
        node_fac = sem("node_fac")
        l_turned = sem("l_turned")
        l_stored = sem("l_stored")
        l_in = sem("l_in")
        l_in_rest = sem("l_in_rest")
        adj_in = [sem("adj_in0"), sem("adj_in1")]
        mask_done = sem("mask_done")
        exp_done = sem("exp_done")
        g_done = sem("g_done")
        ghi_done = sem("ghi_done")
        glo_done = sem("glo_done")
        mm_done = sem("mm_done")
        acc_done = sem("acc_done")
        acc_free = sem("acc_free")
        gate_step = sem("gate_step")
        gate_exp = sem("gate_exp")
        ep_step = sem("ep_step")
        tanh_done = sem("tanh_done")
        sig_done = sem("sig_done")
        fin_done = sem("fin_done")
        res_in = sem("res_in")
        out_done = sem("out_done")
        passed = {nc.scalar.engine: sem("act_passed"), nc.vector.engine: sem("dve_passed"), nc.gpsimd.engine: sem("pool_passed")}

        def apart(eng):
            eng.sem_inc(passed[eng.engine], 1)

        block = top.enter_context(nc.Block())

        xb = x.rearrange("(b p) d -> p b d", p=P)
        ob = out.rearrange("(b p) d -> p b d", p=P)
        adj_v = adjt.rearrange("u p i -> p u i")

        @block.sync
        def _(sp):
            for bank, w in ((0, w_sa), (1, w_gcn)):
                sp.dma_start(wraw[:, :, bank, 0:D], w.rearrange("(c p) n -> p c n", p=P)).then_inc(w_in, 16)
            sp.dma_start(a_bc[:, :, :].rearrange("p c n -> p (c n)"), a_sa.to_broadcast((P, 2 * D))).then_inc(w_in, 16)

            def load_x(b, s):
                sp.dma_start(xin[:, s:s + 2, :], xb[:, bass.ds(b, 2), :]).then_inc(x_in[s // 2], 16)

            load_x(0, 0)
            load_x(2, 2)
            with nc.allow_non_contiguous_dma(reason="four columns of 256 floats"):
                for col, w in ((0, w_a), (1, w_b)):
                    wv = w.rearrange("o (h c p) -> p (o h) c", p=P, c=KC)
                    for c in range(KC):
                        sp.dma_start(wraw[:, c, 1, D + col:D + col + 1], wv[:, 0:1, c]).then_inc(w_in, 16)
                        sp.dma_start(wraw[:, c, 0, D + 2 + col:D + 3 + col], wv[:, 1:2, c]).then_inc(w_in, 16)
            sp.dma_start(bias_bc[:, :], b_gcn.rearrange("(o n) -> o n", o=1).to_broadcast((P, D))).then_inc(w_in, 16)
            sp.dma_start(gate_b[:, 0:1], b_a.rearrange("(o n) -> o n", o=1).to_broadcast((P, 1))).then_inc(w_in, 16)
            sp.dma_start(gate_b[:, 1:2], b_b.rearrange("(o n) -> o n", o=1).to_broadcast((P, 1))).then_inc(w_in, 16)

            def load_adj(u, s):
                sp.dma_start(raw[:, s:s + 2, :], adj_v[:, bass.ds(u, 2), :]).then_inc(adj_in[s // 2], 16)

            load_adj(0, 0)
            load_adj(2, 2)
            with sp.Fori(1, NB // 4) as m:
                for s in (0, 2):
                    sp.wait_ge(xn_done, m * 4 + (s - 2))
                    load_x(m * 4 + s, s)

            sp.wait_ge(acc_free, GB)
            sp.dma_start(sl_dram, lrow[:, :]).then_inc(l_stored, 16)
            sp.wait_ge(l_stored, 16)
            l_flat = sl_dram.rearrange("(o b) p -> o (b p)", o=1)
            lbc_f = lbc[:, :, :].rearrange("p g i -> p (g i)")
            sp.dma_start(lbc_f[:, 0:GW], l_flat[:, 0:GW].to_broadcast((P, GW))).then_inc(l_in, 16)
            sp.dma_start(lbc_f[:, GW:N], l_flat[:, GW:N].to_broadcast((P, N - GW))).then_inc(l_in_rest, 16)
            sp.dma_start(xres[:, :, :], xb[:, 0:GB, :]).then_inc(res_in, 16)

            def adj_body(u):
                for s in (0, 2):
                    sp.wait_ge(mask_done, u + (s - 2))
                    load_adj(u + s, s)

            with sp.Fori(1, NB // 4) as m:
                adj_body(m * 4)
            with sp.Fori(0, NG - 1) as g:
                for q in range(PLEAD // 4 + 1):
                    adj_body(g * NB + (NB + 4 * q))
                sp.wait_ge(fin_done, g + 2)
                sp.dma_start(ob[:, bass.ds(g * GB, GB), :], xres[:, :, :]).then_inc(out_done, 16)
                sp.wait_ge(out_done, g * 16 + 16)
                sp.dma_start(xres[:, :, :], xb[:, bass.ds(g * GB + GB, GB), :]).then_inc(res_in, 16)
                with sp.Fori(PLEAD // 4 + 1, NB // 4) as m:
                    adj_body(g * NB + m * 4 + NB)
            sp.wait_ge(fin_done, NG + 1)
            sp.dma_start(ob[:, (NG - 1) * GB:NG * GB, :], xres[:, :, :]).then_inc(out_done, 16)
            sp.wait_ge(out_done, NG * 16)

        @block.gpsimd
        def _(pool):
            pool.memset(ident[:, :], 0.0).then_inc(const_done, 1)
            pool.memset(wraw[:, :, 1, D + 2:WC], 0.0).then_inc(w_zero, 1)
            pool.memset(half[:, :], -0.5).then_inc(const_done, 1)
            pool.wait_ge(const_done, 2)
            pool.affine_select(out=ident[:, :], in_=ident[:, :], compare_op=ALU.not_equal, fill=1.0,
                               base=0, pattern=[[-1, P]], channel_multiplier=1).then_inc(const_done, 1)

            pool.sem_inc(fin_done, 1)

            def to_rstd(b, s):
                pool.wait_ge(mv_done, b + 1)
                apart(pool)
                pool.tensor_scalar(veps[:, s:s + 1], mv[:, s, 1:2], LN_EPS, None, ALU.add).then_inc(pow_step, 1)
                pool.wait_ge(pow_step, b * 4 + 1)
                pool.tensor_tensor(rstd[:, s:s + 1], veps[:, s:s + 1], half[:, :], ALU.pow).then_inc(pow_step, 1)
                pool.wait_ge(pow_step, b * 4 + 2)
                pool.tensor_tensor(mr[:, s:s + 1], mv[:, s, 0:1], rstd[:, s:s + 1], ALU.mult).then_inc(pow_step, 1)
                pool.wait_ge(pow_step, b * 4 + 3)
                apart(pool)
                pool.tensor_scalar(nmr[:, s:s + 1], mr[:, s:s + 1], -1.0, None, ALU.mult).then_inc(pow_step, 1)

            for b in range(4):
                to_rstd(b, b)
            with pool.Fori(1, NB // 4) as m:
                for s in range(4):
                    pool.wait_ge(xn_done, m * 4 + (s - 3))
                    to_rstd(m * 4 + s, s)

            def to_mask(n, s, first=False):
                if s % 2 == 0:
                    pool.wait_ge(adj_in[s // 2], n * 4 + (16 - 4 * s))
                if not first:
                    pool.wait_ge(mm_done, n - (RING - 1))
                apart(pool)
                pool.tensor_copy(mask[:, s, :], raw[:, s, :]).then_inc(mask_done, 1)

            for n in range(RING):
                to_mask(n, n, True)
            with pool.Fori(1, PLEAD // 4) as m:
                for s in range(4):
                    to_mask(m * 4 + s, s)

            def finish(g):
                pool.wait_ge(tanh_done, g + 1)
                t = stage[:, :, 0, 0:D]
                apart(pool)
                pool.tensor_scalar(t, t, 0.5, 0.5, ALU.mult, ALU.add).then_inc(sig_done, 1)
                pool.wait_ge(sig_done, g + 1)
                pool.wait_ge(res_in, g * 16 + 16)
                pool.tensor_tensor(xres[:, :, :], t, xres[:, :, :], ALU.add).then_inc(fin_done, 1)

            with pool.Fori(0, NG - 1) as g:
                with pool.Fori(PLEAD // 4, NB // 4 + PLEAD // 4) as m:
                    for s in range(4):
                        to_mask(g * NB + m * 4 + s, s)
                finish(g)
            with pool.Fori(PLEAD // 4, NB // 4) as m:
                for s in range(4):
                    to_mask(m * 4 + ((NG - 1) * NB + s), s)
            finish(NG - 1)

        @block.scalar
        def _(act):
            def norm(b, s):
                act.wait_ge(pow_step, b * 4 + 4)
                if not (isinstance(b, int) and b < 2):
                    act.wait_ge(xt_done, b - 1)
                apart(act)
                act.activation(xn[:, s % 2, :], xin[:, s, :], ACT.Identity, bias=nmr[:, s:s + 1],
                               scale=rstd[:, s:s + 1]).then_inc(xn_done, 1)

            def split_x(b, s):
                act.wait_ge(xt_done, b + 1)
                if not (isinstance(b, int) and b < 2):
                    act.wait_ge(feat_done, b - 1)
                act.activation(xt_hi[:, s % 2, :, :], pt[:, s % 2, 0:D].rearrange("p (c n) -> p c n", c=KC),
                               ACT.Relu).then_inc(xhi_done, 1)

            def split_feat(b, s):
                act.wait_ge(feat_done, b + 1)
                apart(act)
                act.activation(feat_hi[:, bass.ds(b, 1), :, :].rearrange("p b t n -> p (b t) n"),
                               pf[:, s % 2, :, 0:WC], ACT.Copy).then_inc(fhi_done, 1)

            norm(0, 0)
            norm(1, 1)
            split_x(0, 0)
            norm(2, 2)
            split_x(1, 1)
            split_feat(0, 0)
            with act.Fori(0, NB // 4 - 1) as m:
                for c in range(1, 5):
                    norm(m * 4 + (c + 2), (c + 2) % 4)
                    split_x(m * 4 + (c + 1), (c + 1) % 4)
                    split_feat(m * 4 + c, c % 4)
            for b in range(NB - 3, NB):
                if b + 2 < NB:
                    norm(b + 2, (b + 2) % 4)
                if b + 1 < NB:
                    split_x(b + 1, (b + 1) % 4)
                split_feat(b, b % 4)

            act.wait_ge(node_step, 1)
            act.activation(cap[:, :], node[:, :, 1], ACT.Exp, scale=-SLOPE).then_inc(node_fac, 1)
            act.activation(cfac[:, :], node[:, :, 0], ACT.Exp, scale=-SLOPE).then_inc(node_fac, 1)
            act.wait_ge(l_turned, 1)
            act.activation(lrow[:, :], pl[0:NB, 0:P], ACT.Copy).then_inc(acc_free, GB)

            def to_exp(n, g, j, s, first=False):
                if not first:
                    act.wait_ge(glo_done, n - (RING - 1))
                apart(act)
                act.activation(e[:, s, :], lbc[:, bass.ds(g, 1), :].rearrange("p g i -> p (g i)"), ACT.Exp,
                               bias=neg_r[:, bass.ds(j, 1)], scale=-(1.0 - SLOPE)).then_inc(exp_done, 1)

            def to_hi(n, s, first=False):
                act.wait_ge(g_done, n + 1)
                if not first:
                    act.wait_ge(mm_done, n - (RING - 1))
                act.activation(g_hi[:, s, :], e[:, s, :], ACT.Copy).then_inc(ghi_done, 1)

            def unit(g, j, s):
                n = g * NB + j
                to_exp(n, g, j, s, first=isinstance(n, int) and n < RING)
                if isinstance(n, int):
                    if n:
                        to_hi(n - 1, (s - 1) % RING, first=n - 1 < RING)
                else:
                    to_hi(n - 1, (s - 1) % RING)

            def move_sums(g):
                act.wait_ge(fin_done, g + 1)
                for ib in range(GB):
                    if ib < GB - 1:
                        act.wait_ge(acc_done, g * (GB - 1) + (ib + 1))
                    else:
                        act.wait_ge(mm_done, g * NB + NB)
                    act.activation(stage[:, ib, :, 0:MC], acc[:, ib, :, 0:MC], ACT.Copy).then_inc(acc_free, 1)
                act.wait_ge(gate_step, g * 9 + 3)
                act.activation(ez[:, :, :], zc[:, :, :], ACT.Exp, scale=-1.0).then_inc(gate_exp, 1)

            def last_sigmoid(g):
                act.wait_ge(ep_step, g * (3 * GB) + 3 * GB)
                t = stage[:, :, 0, 0:D]
                act.activation(t, t, ACT.Tanh, scale=0.5).then_inc(tanh_done, 1)

            act.wait_ge(l_in, 16)
            act.wait_ge(node_step, 2)
            for j in range(LEAD):
                unit(0, j, j % RING)
            act.wait_ge(l_in_rest, 16)
            with act.Fori(0, NG - 1) as g:
                with act.Fori(0, (NB - 1 - LEAD) // 4) as m:
                    for c in range(4):
                        unit(g, m * 4 + (LEAD + c), (LEAD + c) % RING)
                unit(g, NB - 1, (NB - 1) % RING)
                for j in range(3):
                    unit(g + 1, j, j)
                move_sums(g)
                for j in range(3, LEAD):
                    unit(g + 1, j, j % RING)
                last_sigmoid(g)
            with act.Fori(0, (NB - 1 - LEAD) // 4) as m:
                for c in range(4):
                    unit(NG - 1, m * 4 + (LEAD + c), (LEAD + c) % RING)
            unit(NG - 1, NB - 1, (NB - 1) % RING)
            to_hi(NG * NB - 1, RING - 1)
            move_sums(NG - 1)
            last_sigmoid(NG - 1)

        @block.vector
        def _(dve):
            dve.wait_ge(w_in, 16 * (6 + 4 * KC))
            for i in range(2):
                dve.tensor_tensor(wprod[:, :, i, :], wraw[:, :, 0, 0:D],
                                  a_bc[:, i:i + 1, :].to_broadcast((P, KC, D)), ALU.mult).then_inc(w_step, 1)
            dve.wait_ge(w_step, 2)
            dve.tensor_reduce(out=wraw[:, :, 0, D:D + 2], in_=wprod[:, :, :, :], axis=AX_X, op=ALU.add).then_inc(w_step, 1)
            dve.wait_ge(w_step, 3)
            dve.wait_ge(w_zero, 1)
            dve.tensor_copy(w_hi[:, :, :, :], wraw[:, :, :, :]).then_inc(w_step, 1)
            dve.wait_ge(w_step, 4)
            flat = "p c t n -> p (c t n)"
            dve.tensor_tensor(w_lo[:, :, :, :].rearrange(flat), wraw[:, :, :, :].rearrange(flat),
                              w_hi[:, :, :, :].bitcast(F32).rearrange(flat), ALU.subtract).then_inc(w_ready, 1)

            def stat(b, s):
                if s % 2 == 0:
                    dve.wait_ge(x_in[s // 2], b * 4 + (16 - 4 * s))
                if not (isinstance(b, int) and b < 4):
                    dve.wait_ge(pow_step, b * 4 - 12)
                dve.bn_stats(stats[:, s, :], xin[:, s, :]).then_inc(stat_done, 1)
                dve.wait_ge(stat_done, b + 1)
                apart(dve)
                dve.bn_aggr(mv[:, s, :], stats[:, s, :]).then_inc(mv_done, 1)

            def rest_x(b, s):
                dve.wait_ge(xhi_done, b + 1)
                dve.scalar_tensor_tensor(
                    out=xt_lo[:, s % 2, :, :].rearrange("p c n -> p (c n)"), in0=pt[:, s % 2, 0:D], scalar=0.0,
                    in1=xt_hi[:, s % 2, :, :].bitcast(F32).rearrange("p c n -> p (c n)"),
                    op0=ALU.max, op1=ALU.subtract).then_inc(xlo_done, 1)

            def rest_feat(b, s):
                dve.wait_ge(fhi_done, b + 1)
                dve.tensor_tensor(feat_lo[:, bass.ds(b, 1), :, :].rearrange("p b t n -> p (b t) n"),
                                  pf[:, s % 2, :, 0:WC],
                                  feat_hi[:, bass.ds(b, 1), :, :].bitcast(F32).rearrange("p b t n -> p (b t) n"),
                                  ALU.subtract).then_inc(flo_done, 1)

            for b in range(3):
                stat(b, b)
            rest_x(0, 0)
            stat(3, 3)
            rest_x(1, 1)
            rest_feat(0, 0)
            with dve.Fori(0, NB // 4 - 1) as m:
                for c in range(1, 5):
                    stat(m * 4 + (c + 3), (c + 3) % 4)
                    rest_x(m * 4 + (c + 1), (c + 1) % 4)
                    rest_feat(m * 4 + c, c % 4)
            for b in range(NB - 3, NB):
                if b + 1 < NB:
                    rest_x(b + 1, (b + 1) % 4)
                rest_feat(b, b % 4)

            dve.wait_ge(flo_done, NB)
            dve.tensor_tensor(node[:, :, :], feat_hi[:, :, 0, D:WC].bitcast(F32), feat_lo[:, :, 0, D:WC].bitcast(F32),
                              ALU.add).then_inc(node_step, 1)
            dve.wait_ge(node_step, 1)
            dve.tensor_scalar(neg_r[:, :], node[:, :, 1], -1.0, None, ALU.mult).then_inc(node_step, 1)
            dve.tensor_copy(lcol[:, :], node[:, :, 0]).then_inc(node_step, 1)
            dve.memset(feat_hi[:, :, 0, D:D + 1].bitcast(F32), 1.0).then_inc(node_step, 1)
            dve.memset(feat_hi[:, :, 0, D + 1:D + 2].bitcast(F32), 0.0).then_inc(node_step, 1)
            dve.memset(feat_lo[:, :, 0, D:D + 2].bitcast(F32), 0.0).then_inc(node_step, 1)
            dve.tensor_tensor(node[:, :, 2:4], node[:, :, 2:4],
                              gate_b[:, :].rearrange("p (o c) -> p o c", o=1).to_broadcast((P, NB, 2)), ALU.add).then_inc(node_step, 1)

            def to_g(n, j, s):
                dve.wait_ge(exp_done, n + 1)
                dve.wait_ge(mask_done, n + 1)
                dve.scalar_tensor_tensor(out=e[:, s, :], in0=e[:, s, :], scalar=cap[:, bass.ds(j, 1)],
                                         in1=mask[:, s, :].bitcast(F32), op0=ALU.min, op1=ALU.mult).then_inc(g_done, 1)

            def to_lo(n, s):
                dve.wait_ge(ghi_done, n + 1)
                dve.tensor_tensor(g_lo[:, s, :], e[:, s, :], g_hi[:, s, :].bitcast(F32), ALU.subtract).then_inc(glo_done, 1)

            def unit(g, j, s):
                n = g * NB + j
                to_g(n, j, s)
                if not isinstance(n, int) or n:
                    to_lo(n - 1, (s - 1) % RING)

            def small_steps(g):
                k = g * 9
                dve.wait_ge(acc_free, g * GB + 2 * GB)
                rows = bass.ds(g * GB, GB)
                dve.tensor_tensor(z[:, :, :], stage[:, :, 1, D:D + 2], node[:, rows, 2:4], ALU.add).then_inc(gate_step, 1)
                dve.tensor_tensor(dn[:, :], stage[:, :, 0, D], cfac[:, rows], ALU.mult).then_inc(gate_step, 1)
                dve.wait_ge(gate_step, k + 1)
                dve.tensor_scalar(zc[:, :, :], z[:, :, :], Z_MIN, None, ALU.max).then_inc(gate_step, 1)
                dve.wait_ge(gate_step, k + 2)
                dve.tensor_scalar(dn1[:, :], dn[:, :], DEN_EPS, None, ALU.add).then_inc(gate_step, 1)
                dve.wait_ge(gate_step, k + 4)
                dve.reciprocal(rdn[:, :], dn1[:, :]).then_inc(gate_step, 1)
                dve.wait_ge(gate_step, k + 5)
                dve.tensor_tensor(crdn[:, :], rdn[:, :], cfac[:, rows], ALU.mult).then_inc(gate_step, 1)
                dve.wait_ge(gate_exp, g + 1)
                dve.tensor_scalar(ez1[:, :, :], ez[:, :, :], 1.0, None, ALU.add).then_inc(gate_step, 1)
                dve.wait_ge(gate_step, k + 7)
                dve.reciprocal(gate[:, :, :], ez1[:, :, :]).then_inc(gate_step, 1)
                dve.wait_ge(gate_step, k + 8)
                dve.tensor_tensor(ca[:, :], crdn[:, :], gate[:, :, 0], ALU.mult).then_inc(gate_step, 1)

            def wide_steps(g, ib):
                k = g * (3 * GB) + 3 * ib
                v = stage[:, ib, 1, 0:D]
                dve.tensor_tensor(v, v, bias_bc[:, :], ALU.add).then_inc(ep_step, 1)
                dve.wait_ge(ep_step, k + 1)
                dve.tensor_scalar(v, v, gate[:, ib, 1:2], None, ALU.mult).then_inc(ep_step, 1)
                dve.wait_ge(ep_step, k + 2)
                if ib == 0:
                    dve.wait_ge(gate_step, g * 9 + 9)
                y = stage[:, ib, 0, 0:D]
                dve.scalar_tensor_tensor(out=y, in0=y, scalar=ca[:, ib:ib + 1], in1=v,
                                         op0=ALU.mult, op1=ALU.add).then_inc(ep_step, 1)

            dve.wait_ge(node_fac, 2)
            dve.wait_ge(node_step, 7)
            for j in range(LEAD):
                unit(0, j, j % RING)
            with dve.Fori(0, NG - 1) as g:
                with dve.Fori(0, (NB - 1 - LEAD) // 4) as m:
                    for c in range(4):
                        unit(g, m * 4 + (LEAD + c), (LEAD + c) % RING)
                unit(g, NB - 1, (NB - 1) % RING)
                for j in range(3):
                    unit(g + 1, j, j)
                small_steps(g)
                for j in range(3, LEAD):
                    unit(g + 1, j, j % RING)
                    wide_steps(g, j - 3)
            with dve.Fori(0, (NB - 1 - LEAD) // 4) as m:
                for c in range(4):
                    unit(NG - 1, m * 4 + (LEAD + c), (LEAD + c) % RING)
            unit(NG - 1, NB - 1, (NB - 1) % RING)
            to_lo(NG * NB - 1, RING - 1)
            small_steps(NG - 1)
            for ib in range(GB):
                wide_steps(NG - 1, ib)

        @block.tensor
        def _(pe):
            def turn(b, s):
                pe.wait_ge(xn_done, b + 1)
                if not (isinstance(b, int) and b < 2):
                    pe.wait_ge(xlo_done, b - 1)
                for c in range(KC):
                    mm = pe.transpose(pt[:, s % 2, c * P:(c + 1) * P], xn[:, s % 2, c * P:(c + 1) * P], ident[:, :])
                mm.then_inc(xt_done, 1)

            def features(b, s):
                pe.wait_ge(xlo_done, b + 1)
                if not (isinstance(b, int) and b < 2):
                    pe.wait_ge(flo_done, b - 1)
                for t in range(2):
                    parts = [(xa, wa, c) for c in range(KC) for xa, wa in ((xt_hi, w_hi), (xt_hi, w_lo), (xt_lo, w_hi))]
                    for i, (xa, wa, c) in enumerate(parts):
                        mm = pe.matmul(pf[:, s % 2, t, 0:WC], xa[:, s % 2, c, :], wa[:, c, t, :],
                                       start=(i == 0), stop=(i == len(parts) - 1))
                mm.then_inc(feat_done, 1)

            pe.wait_ge(const_done, 3)
            turn(0, 0)
            pe.wait_ge(w_ready, 1)
            turn(1, 1)
            features(0, 0)
            turn(2, 2)
            features(1, 1)
            with pe.Fori(0, NB // 4 - 1) as m:
                for c in range(2, 6):
                    turn(m * 4 + (c + 1), (c + 1) % 4)
                    features(m * 4 + c, c % 4)
            for b in range(NB - 2, NB):
                if b + 1 < NB:
                    turn(b + 1, (b + 1) % 4)
                features(b, b % 4)
            pe.wait_ge(node_step, 3)
            pe.transpose(pl[0:NB, 0:P], lcol[:, :], ident[:, :]).then_inc(l_turned, 1)

            def unit(g, j, s, first=False, last=False):
                n = g * NB + j
                pe.wait_ge(mask_done, n + 1)
                pe.wait_ge(glo_done, n + 1)

                def part(f, t):
                    return f[:, bass.ds(j, 1), t, 0:MC].rearrange("p b n -> p (b n)")
                for ib in range(GB):
                    cols = slice(ib * P, (ib + 1) * P)
                    if first:
                        pe.wait_ge(acc_free, g * GB + (ib + 1))
                    for i, (lhs, f) in enumerate(((mask, feat_hi), (mask, feat_lo))):
                        mm = pe.matmul(acc[:, ib, 1, 0:MC], lhs[:, s, cols], part(f, 1),
                                       start=(first and i == 0), stop=(last and i == 1))
                    for i, (lhs, f) in enumerate(((g_hi, feat_hi), (g_hi, feat_lo), (g_lo, feat_hi))):
                        mm = pe.matmul(acc[:, ib, 0, 0:MC], lhs[:, s, cols], part(f, 0),
                                       start=(first and i == 0), stop=(last and i == 2))
                    if last and ib < GB - 1:
                        mm.then_inc(acc_done, 1)
                mm.then_inc(mm_done, 1)

            pe.wait_ge(node_step, 7)
            with pe.Fori(0, NG) as g:
                unit(g, 0, 0, first=True)
                for j in range(1, 3):
                    unit(g, j, j)
                with pe.Fori(0, (NB - 4) // 4) as m:
                    for c in range(4):
                        unit(g, m * 4 + (c + 3), (c + 3) % RING)
                unit(g, NB - 1, RING - 1, last=True)


_INS = ["x", "adjt", "w_sa", "a_sa", "w_gcn", "b_gcn", "w_a", "b_a", "w_b", "b_b"]


def kernel(x, adj, L0_gnn_W_sa, L0_gnn_a_sa, L0_gnn_W_gcnb, L0_gnn_b_gcnb, L0_gnn_Wa, L0_gnn_ba, L0_gnn_Wb, L0_gnn_bb):
    import concourse.bacc as _bacc
    from concourse.bass_utils import run_bass_kernel_spmd as _run

    n = x.shape[0]
    adjt = np.asarray(adj).reshape(n // GW, GW, n // P, P).transpose(0, 2, 3, 1).reshape(-1, P, GW)
    values = [x, adjt, L0_gnn_W_sa, L0_gnn_a_sa, L0_gnn_W_gcnb, L0_gnn_b_gcnb, L0_gnn_Wa, L0_gnn_ba, L0_gnn_Wb, L0_gnn_bb]
    nc = _bacc.Bacc("TRN2", target_bir_lowering=False, num_devices=1)
    arrays, args = {}, []
    for name, v in zip(_INS, values):
        a = np.ascontiguousarray(v)
        arrays[f"in_{name}"] = a
        args.append(nc.dram_tensor(f"in_{name}", a.shape, mybir.dt.from_np(a.dtype), kind="ExternalInput").ap())
    args.append(nc.dram_tensor("out_0", (n, x.shape[1]), F32, kind="ExternalOutput").ap())
    build(nc, *args)
    r = _run(nc, [arrays], core_ids=[0])
    return r.results[0]["out_0"]
```

```python
from contextlib import ExitStack

import numpy as np

import concourse.bass as bass
from concourse import mybir

F32 = mybir.dt.float32
F32R = mybir.dt.float32r
ALU = mybir.AluOpType
ACT = mybir.ActivationFunctionType
AX_X = mybir.AxisListType.X

P = 128
GB = 4
GW = GB * P
SLOPE = 0.01
LN_EPS = 1e-5
DEN_EPS = 1e-5
Z_MIN = -88.0
RING = 4


def build(nc, x, adjt, weights, a_sa, biases, out):
    N, D = x.shape
    NB = N // P
    NG = N // GW
    KC = D // P
    WC = D + 4
    FC = 2 + WC
    MC = D + 2
    START = (0, 2)
    AB = 8
    XS = 4
    TAIL = 1 + (NB - 1) // AB * AB
    LEAD = 11
    PLEAD = 16
    assert NB % RING == 0 and NB >= PLEAD + RING and (NB - 1 - LEAD) % RING == 0 and D == 2 * P

    sl_dram = nc.dram_tensor("sl_scratch", [NB, P], F32, kind="Internal").ap()

    with ExitStack() as top:
        def sem(name):
            return top.enter_context(nc.semaphore(name))

        def sbuf(stack, name, shape, dt):
            return stack.enter_context(nc.sbuf_tensor(name, shape, dt))

        def psum(stack, name, shape, dt):
            return stack.enter_context(nc.psum_tensor(name, shape, dt))

        feat_hi = sbuf(top, "feat_hi", [P, NB, 2, FC], F32R)
        feat_lo = sbuf(top, "feat_lo", [P, NB, 2, FC], F32R)
        raw = sbuf(top, "raw", [P, RING, GW], F32)
        mask = sbuf(top, "mask", [P, RING, GW], F32R)
        e = sbuf(top, "e", [P, RING, GW], F32)
        g_hi = sbuf(top, "g_hi", [P, RING, GW], F32R)
        g_lo = sbuf(top, "g_lo", [P, RING, GW], F32R)
        lr = sbuf(top, "lr", [P, NB, 2], F32)
        own = sbuf(top, "own", [P, NB, 2], F32)
        cap = sbuf(top, "cap", [P, NB], F32)
        cfac = sbuf(top, "cfac", [P, NB], F32)
        bias_bc = sbuf(top, "bias_bc", [P, D + 2], F32)

        pa = ExitStack()
        xin = sbuf(pa, "xin", [P, AB, D], F32)
        xn = sbuf(pa, "xn", [P, 2, D], F32)
        ident = sbuf(pa, "ident", [P, P], F32)
        wprod = sbuf(pa, "wprod", [P, D], F32)
        wraw = sbuf(pa, "wraw", [P, KC, 2, WC], F32)
        w_hi = sbuf(pa, "w_hi", [P, KC, 2, WC], F32R)
        w_lo = sbuf(pa, "w_lo", [P, KC, 2, WC], F32R)
        xt_hi = sbuf(pa, "xt_hi", [P, XS, KC, P], F32R)
        xt_lo = sbuf(pa, "xt_lo", [P, XS, KC, P], F32R)
        a_bc = sbuf(pa, "a_bc", [P, 2, D], F32)
        stats = sbuf(pa, "stats", [P, AB, 6], F32)
        mv = sbuf(pa, "mv", [P, AB, 2], F32)
        half = sbuf(pa, "half", [P, 4], F32)
        veps = sbuf(pa, "veps", [P, AB], F32)
        rstd = sbuf(pa, "rstd", [P, AB], F32)
        mr = sbuf(pa, "mr", [P, AB], F32)
        nmr = sbuf(pa, "nmr", [P, AB], F32)
        pt = psum(pa, "pt", [P, 2, 512], F32)
        pf = psum(pa, "pf", [P, 2, 2, 512], F32)
        pa.close()

        stage = sbuf(top, "stage", [P, GB, 2, FC], F32)
        xres = sbuf(top, "xres", [P, GB, D], F32)
        lbc = sbuf(top, "lbc", [P, NG, GW], F32)
        z = sbuf(top, "z", [P, GB, 2], F32)
        zc = sbuf(top, "zc", [P, GB, 2], F32)
        ez = sbuf(top, "ez", [P, GB, 2], F32)
        ez1 = sbuf(top, "ez1", [P, GB, 2], F32)
        gate = sbuf(top, "gate", [P, GB, 2], F32)
        dn = sbuf(top, "dn", [P, GB], F32)
        dn1 = sbuf(top, "dn1", [P, GB], F32)
        rdn = sbuf(top, "rdn", [P, GB], F32)
        crdn = sbuf(top, "crdn", [P, GB], F32)
        ca = sbuf(top, "ca", [P, GB], F32)
        acc = psum(top, "acc", [P, GB, 2, 512], F32)

        w_in = sem("w_in")
        a_in = sem("a_in")
        bias_in = sem("bias_in")
        x_in = [sem(f"x_in{i}") for i in range(AB // 2)]
        const_done = sem("const_done")
        ones_set = sem("ones_set")
        w_step = sem("w_step")
        w_hi_done = sem("w_hi_done")
        w_ready = sem("w_ready")
        stat_done = sem("stat_done")
        mv_done = sem("mv_done")
        pow_step = sem("pow_step")
        xn_done = sem("xn_done")
        xt_done = sem("xt_done")
        xhi_done = sem("xhi_done")
        xlo_done = sem("xlo_done")
        feat_done = sem("feat_done")
        fhi_done = sem("fhi_done")
        flo_done = sem("flo_done")
        lr_done = sem("lr_done")
        own_done = sem("own_done")
        cap_done = sem("cap_done")
        cfac_done = sem("cfac_done")
        l_stored = sem("l_stored")
        l_stored_rest = sem("l_stored_rest")
        l_in = sem("l_in")
        adj_in = [sem("adj_in0"), sem("adj_in1")]
        mask_done = sem("mask_done")
        exp_done = sem("exp_done")
        g_done = sem("g_done")
        ghi_done = sem("ghi_done")
        glo_done = sem("glo_done")
        mm_done = sem("mm_done")
        acc_done = sem("acc_done")
        acc_free = sem("acc_free")
        gate_step = sem("gate_step")
        gate_exp = sem("gate_exp")
        ep_step = sem("ep_step")
        y_done = sem("y_done")
        tanh_done = sem("tanh_done")
        sig_done = sem("sig_done")
        fin_done = sem("fin_done")
        res_in = sem("res_in")
        out_done = sem("out_done")
        passed = {nc.scalar.engine: sem("act_passed"), nc.vector.engine: sem("dve_passed"), nc.gpsimd.engine: sem("pool_passed")}

        def apart(eng):
            eng.sem_inc(passed[eng.engine], 1)

        def scales_of(m, k):
            if isinstance(m, int) and m == 0 and k < 4:
                return 4 * (k // 2 + 1)
            return m * AB + 4 * (k // 4 + 2)

        block = top.enter_context(nc.Block())

        xb = x.rearrange("(b p) d -> p b d", p=P)
        ob = out.rearrange("(b p) d -> p b d", p=P)
        adj_v = adjt.rearrange("u p i -> p u i")

        @block.sync
        def _(sp):
            def load_x(b, s):
                sp.dma_start(xin[:, s:s + 2, :], xb[:, bass.ds(b, 2), :]).then_inc(x_in[s // 2], 16)

            def load_adj(u, s):
                sp.dma_start(raw[:, s:s + 2, :], adj_v[:, bass.ds(u, 2), :]).then_inc(adj_in[s // 2], 16)

            for s in range(0, AB, 2):
                load_x(s, s)
            load_adj(0, 0)
            load_adj(2, 2)
            sp.dma_start(bias_bc[:, :], biases.to_broadcast((P, D + 2))).then_inc(bias_in, 16)
            with sp.Fori(1, NB // AB) as m:
                for s in range(0, AB, 2):
                    sp.wait_ge(xn_done, m * AB + (s + 2 - AB))
                    load_x(m * AB + s, s)

            l_flat = sl_dram.rearrange("(o b) p -> o (b p)", o=1)
            l_col = sl_dram.rearrange("b p -> p b")
            lbc_f = lbc[:, :, :].rearrange("p g i -> p (g i)")
            with nc.allow_non_contiguous_dma(reason="a column of l a block: 16 KB in all"):
                sp.wait_ge(lr_done, 1)
                sp.dma_start(l_col[:, 0:GB], lr[:, 0:GB, 0]).then_inc(l_stored, 16)
                sp.wait_ge(l_stored, 16)
                sp.dma_start(lbc_f[:, 0:GW], l_flat[:, 0:GW].to_broadcast((P, GW))).then_inc(l_in, 16)
                sp.wait_ge(lr_done, 2)
                sp.dma_start(l_col[:, GB:NB], lr[:, GB:NB, 0]).then_inc(l_stored_rest, 16)

            def adj_body(u):
                for s in (0, 2):
                    sp.wait_ge(mask_done, u + (s - 2))
                    load_adj(u + s, s)

            adj_body(4)
            sp.wait_ge(feat_done, NB)
            sp.dma_start(xres[:, :, :], xb[:, 0:GB, :]).then_inc(res_in, 16)
            with sp.Fori(2, NB // 4) as m:
                adj_body(m * 4)
            sp.wait_ge(l_stored_rest, 16)
            with sp.Fori(0, NG - 1) as g:
                sp.dma_start(lbc_f[:, bass.ds(g * GW + GW, GW)],
                             l_flat[:, bass.ds(g * GW + GW, GW)].to_broadcast((P, GW))).then_inc(l_in, 16)
                for q in range(PLEAD // 4 + 1):
                    adj_body(g * NB + (NB + 4 * q))
                sp.wait_ge(fin_done, g + 2)
                sp.dma_start(ob[:, bass.ds(g * GB, GB), :], xres[:, :, :]).then_inc(out_done, 16)
                sp.wait_ge(out_done, g * 16 + 16)
                sp.dma_start(xres[:, :, :], xb[:, bass.ds(g * GB + GB, GB), :]).then_inc(res_in, 16)
                with sp.Fori(PLEAD // 4 + 1, NB // 4) as m:
                    adj_body(g * NB + m * 4 + NB)
            for ib in range(GB):
                sp.wait_ge(fin_done, NG + 1 + ib)
                sp.dma_start(ob[:, (NG - 1) * GB + ib, :], xres[:, ib, :]).then_inc(out_done, 16)
            sp.wait_ge(out_done, (NG - 1 + GB) * 16)

        @block.gpsimd
        def _(pool):
            pool.memset(half[:, :], -0.5).then_inc(const_done, 1)
            pool.memset(ident[:, :], 0.0).then_inc(const_done, 1)
            pool.wait_ge(const_done, 2)
            pool.affine_select(out=ident[:, :], in_=ident[:, :], compare_op=ALU.not_equal, fill=1.0,
                               base=0, pattern=[[-1, P]], channel_multiplier=1).then_inc(const_done, 1)
            pool.sem_inc(fin_done, 1)

            def to_rstd(q, b, s, n):
                pool.wait_ge(mv_done, b + n)
                if not isinstance(b, int):
                    pool.wait_ge(xn_done, b + (n - AB))
                apart(pool)
                r = slice(s, s + n)
                pool.tensor_scalar(veps[:, r], mv[:, r, 1], LN_EPS, None, ALU.add).then_inc(pow_step, 1)
                pool.wait_ge(pow_step, q * 4 + 1)
                pool.tensor_tensor(rstd[:, r], veps[:, r], half[:, 0:n], ALU.pow).then_inc(pow_step, 1)
                pool.wait_ge(pow_step, q * 4 + 2)
                pool.tensor_tensor(mr[:, r], mv[:, r, 0], rstd[:, r], ALU.mult).then_inc(pow_step, 1)
                pool.wait_ge(pow_step, q * 4 + 3)
                apart(pool)
                pool.tensor_scalar(nmr[:, r], mr[:, r], -1.0, None, ALU.mult).then_inc(pow_step, 1)

            to_rstd(0, 0, 0, 2)
            pool.memset(feat_hi[:, :, 0, 0:1].bitcast(F32), 1.0).then_inc(ones_set, 1)
            pool.memset(feat_hi[:, :, 0, 1:2].bitcast(F32), 0.0).then_inc(ones_set, 1)
            to_rstd(1, 2, 2, 2)
            to_rstd(2, 4, 4, 4)
            with pool.Fori(1, NB // AB) as m:
                for h in range(AB // 4):
                    to_rstd(m * (AB // 4) + (h + 1), m * AB + 4 * h, 4 * h, 4)

            def to_mask(n, s, first=False):
                if s % 2 == 0:
                    pool.wait_ge(adj_in[s // 2], n * 4 + (16 - 4 * s))
                if not first:
                    pool.wait_ge(mm_done, n - (RING - 1))
                apart(pool)
                pool.tensor_scalar(mask[:, s, :], raw[:, s, :], 1.0, 0.0, ALU.mult, ALU.add).then_inc(mask_done, 1)

            for n in range(RING):
                to_mask(n, n, True)
            with pool.Fori(1, PLEAD // 4) as m:
                for s in range(4):
                    to_mask(m * 4 + s, s)

            def finish(g, ibs, k):
                pool.wait_ge(tanh_done, g + (k + 1))
                t = stage[:, ibs, 0, 2:MC]
                apart(pool)
                pool.tensor_scalar(t, t, 0.5, 0.5, ALU.mult, ALU.add).then_inc(sig_done, 1)
                pool.wait_ge(sig_done, g + (k + 1))
                if k == 0:
                    pool.wait_ge(res_in, g * 16 + 16)
                pool.tensor_tensor(xres[:, ibs, :], t, xres[:, ibs, :], ALU.add).then_inc(fin_done, 1)

            with pool.Fori(0, NG - 1) as g:
                with pool.Fori(PLEAD // 4, NB // 4 + PLEAD // 4) as m:
                    for s in range(4):
                        to_mask(g * NB + m * 4 + s, s)
                finish(g, slice(0, GB), 0)
            with pool.Fori(PLEAD // 4, NB // 4) as m:
                for s in range(4):
                    to_mask(m * 4 + ((NG - 1) * NB + s), s)
            for ib in range(GB):
                finish(NG - 1, ib, ib)

        @block.scalar
        def _(act):
            act.dma_start(wraw[:, :, :, :].rearrange("p c t n -> p (c t n)"), weights).then_inc(w_in, 16)
            act.dma_start(a_bc[:, :, :].rearrange("p c n -> p (c n)"), a_sa.to_broadcast((P, 2 * D))).then_inc(a_in, 16)

            def norm(b, s, scales):
                act.wait_ge(pow_step, scales)
                if not (isinstance(b, int) and b < 2):
                    act.wait_ge(xt_done, b - 1)
                apart(act)
                act.activation(xn[:, s % 2, :], xin[:, s, :], ACT.Identity, bias=nmr[:, s:s + 1],
                               scale=rstd[:, s:s + 1]).then_inc(xn_done, 1)

            def split_x(b, s):
                act.wait_ge(xt_done, b + 1)
                if not (isinstance(b, int) and b < XS):
                    act.wait_ge(feat_done, b - (XS - 1))
                act.activation(xt_hi[:, s % XS, :, :], pt[:, s % 2, 0:D].rearrange("p (c n) -> p c n", c=KC),
                               ACT.Relu).then_inc(xhi_done, 1)

            def split_feat(b, s):
                act.wait_ge(feat_done, b + 1)
                apart(act)
                act.activation(feat_hi[:, bass.ds(b, 1), :, 2:FC].rearrange("p b t n -> p (b t) n"),
                               pf[:, s % 2, :, 0:WC], ACT.Copy).then_inc(fhi_done, 1)

            def to_exp(n, g, j, s, first=False):
                if not first:
                    act.wait_ge(glo_done, n - (RING - 1))
                apart(act)
                act.activation(e[:, s, :], lbc[:, bass.ds(g, 1), :].rearrange("p g i -> p (g i)"), ACT.Exp,
                               bias=lr[:, bass.ds(j, 1), 1], scale=-(1.0 - SLOPE)).then_inc(exp_done, 1)

            def to_hi(n, s, first=False):
                act.wait_ge(g_done, n + 1)
                if not first:
                    act.wait_ge(mm_done, n - (RING - 1))
                act.activation(g_hi[:, s, :], e[:, s, :], ACT.Copy).then_inc(ghi_done, 1)

            def unit(g, j, s):
                n = g * NB + j
                to_exp(n, g, j, s, first=isinstance(n, int) and n < RING)
                to_hi(n - 1, (s - 1) % RING, first=isinstance(n, int) and n - 1 < RING)

            def move_sums(g):
                act.wait_ge(fin_done, g + 1)
                for ib in range(GB):
                    if ib < GB - 1:
                        act.wait_ge(acc_done, g * (GB - 1) + (ib + 1))
                    else:
                        act.wait_ge(mm_done, g * NB + NB)
                    act.activation(stage[:, ib, :, 0:MC], acc[:, ib, :, 0:MC], ACT.Copy).then_inc(acc_free, 1)
                act.wait_ge(gate_step, g * 9 + 3)
                act.activation(ez[:, :, :], zc[:, :, :], ACT.Exp, scale=-1.0).then_inc(gate_exp, 1)

            def last_sigmoid(g, ibs, k):
                act.wait_ge(y_done, g * GB + (k + 1 if ibs == k else GB))
                t = stage[:, ibs, 0, 2:MC]
                act.activation(t, t, ACT.Tanh, scale=0.5).then_inc(tanh_done, 1)

            for b in range(3):
                norm(b, b, scales_of(0, b))
                if b:
                    split_x(b - 1, b - 1)
                if b == 0:
                    act.wait_ge(w_in, 16)
                    act.activation(w_hi[:, :, 0, 0:D], wraw[:, :, 0, 0:D], ACT.Copy).then_inc(w_hi_done, 1)
                    act.activation(w_hi[:, :, 1, :], wraw[:, :, 1, :], ACT.Copy).then_inc(w_hi_done, 1)
            norm(3, 3, scales_of(0, 3))
            split_x(2, 2)
            split_feat(0, 0)
            norm(4, 4, scales_of(0, 4))
            split_x(3, 3)
            split_feat(1, 1)
            with act.Fori(0, TAIL // AB) as m:
                for c in range(2, AB + 2):
                    norm(m * AB + (c + 3), (c + 3) % AB, scales_of(m, c + 3))
                    split_x(m * AB + (c + 2), (c + 2) % AB)
                    split_feat(m * AB + c, c % AB)
            for b in range(TAIL + 1, NB):
                if b + 3 < NB:
                    norm(b + 3, (b + 3) % AB, scales_of(0, b + 3))
                if b + 2 < NB:
                    split_x(b + 2, (b + 2) % AB)
                if b == TAIL + 1:
                    act.wait_ge(lr_done, 1)
                    act.activation(cap[:, 0:TAIL - 1], lr[:, 0:TAIL - 1, 1], ACT.Exp, scale=SLOPE).then_inc(cap_done, 1)
                if b == NB - 3:
                    act.wait_ge(l_in, 16)
                    to_exp(0, 0, 0, 0, first=True)
                if b == NB - 2:
                    unit(0, 1, 1)
                split_feat(b, b % AB)
            unit(0, 2, 2)
            act.wait_ge(lr_done, 2)
            act.activation(cap[:, TAIL - 1:NB], lr[:, TAIL - 1:NB, 1], ACT.Exp, scale=SLOPE).then_inc(cap_done, 1)
            act.activation(cfac[:, :], lr[:, :, 0], ACT.Exp, scale=-SLOPE).then_inc(cfac_done, 1)
            for j in range(3, LEAD):
                unit(0, j, j % RING)
            with act.Fori(0, NG - 1) as g:
                with act.Fori(0, (NB - 1 - LEAD) // 4) as m:
                    for c in range(4):
                        unit(g, m * 4 + (LEAD + c), (LEAD + c) % RING)
                unit(g, NB - 1, (NB - 1) % RING)
                act.wait_ge(l_in, g * 16 + 32)
                for j in range(3):
                    unit(g + 1, j, j)
                move_sums(g)
                for j in range(3, LEAD):
                    unit(g + 1, j, j % RING)
                last_sigmoid(g, slice(0, GB), 0)
            with act.Fori(0, (NB - 1 - LEAD) // 4) as m:
                for c in range(4):
                    unit(NG - 1, m * 4 + (LEAD + c), (LEAD + c) % RING)
            unit(NG - 1, NB - 1, (NB - 1) % RING)
            to_hi(NG * NB - 1, RING - 1)
            move_sums(NG - 1)
            for ib in range(GB):
                last_sigmoid(NG - 1, ib, ib)

        @block.vector
        def _(dve):
            def stat(b, s, arrived, last=None):
                if s % 2 == 0:
                    dve.wait_ge(x_in[s // 2], arrived)
                if last is not None:
                    dve.wait_ge(pow_step, last)
                dve.bn_stats(stats[:, s, :], xin[:, s, :]).then_inc(stat_done, 1)
                dve.wait_ge(stat_done, b + 1)
                apart(dve)
                dve.bn_aggr(mv[:, s, :], stats[:, s, :]).then_inc(mv_done, 1)

            def rest_x(b, s):
                dve.wait_ge(xhi_done, b + 1)
                dve.scalar_tensor_tensor(
                    out=xt_lo[:, s % XS, :, :].rearrange("p c n -> p (c n)"), in0=pt[:, s % 2, 0:D], scalar=0.0,
                    in1=xt_hi[:, s % XS, :, :].bitcast(F32).rearrange("p c n -> p (c n)"),
                    op0=ALU.max, op1=ALU.subtract).then_inc(xlo_done, 1)

            def rest_feat(b, s):
                dve.wait_ge(fhi_done, b + 1)
                dve.tensor_tensor(feat_lo[:, bass.ds(b, 1), :, 2:FC].rearrange("p b t n -> p (b t) n"),
                                  pf[:, s % 2, :, 0:WC],
                                  feat_hi[:, bass.ds(b, 1), :, 2:FC].bitcast(F32).rearrange("p b t n -> p (b t) n"),
                                  ALU.subtract).then_inc(flo_done, 1)

            def whole(out, f, b0, b1, t, c):
                return dve.tensor_tensor(out[:, b0:b1, :], f[0][:, b0:b1, t, c:c + 2].bitcast(F32),
                                         f[1][:, b0:b1, t, c:c + 2].bitcast(F32), ALU.add)

            def to_g(n, j, s):
                dve.wait_ge(exp_done, n + 1)
                dve.wait_ge(mask_done, n + 1)
                dve.scalar_tensor_tensor(out=e[:, s, :], in0=e[:, s, :], scalar=cap[:, bass.ds(j, 1)],
                                         in1=mask[:, s, :].bitcast(F32), op0=ALU.min, op1=ALU.mult).then_inc(g_done, 1)

            def to_lo(n, s):
                dve.wait_ge(ghi_done, n + 1)
                dve.tensor_tensor(g_lo[:, s, :], e[:, s, :], g_hi[:, s, :].bitcast(F32), ALU.subtract).then_inc(glo_done, 1)

            def unit(g, j, s):
                n = g * NB + j
                to_g(n, j, s)
                to_lo(n - 1, (s - 1) % RING)

            def small_steps(g):
                k = g * 9
                dve.wait_ge(acc_free, g * GB + GB)
                rows = bass.ds(g * GB, GB)
                dve.tensor_tensor(z[:, :, :], stage[:, :, 1, D:D + 2], own[:, rows, :], ALU.add).then_inc(gate_step, 1)
                dve.tensor_tensor(dn[:, :], stage[:, :, 0, 0], cfac[:, rows], ALU.mult).then_inc(gate_step, 1)
                dve.wait_ge(gate_step, k + 1)
                dve.tensor_scalar(zc[:, :, :], z[:, :, :], Z_MIN, None, ALU.max).then_inc(gate_step, 1)
                dve.wait_ge(gate_step, k + 2)
                dve.tensor_scalar(dn1[:, :], dn[:, :], DEN_EPS, None, ALU.add).then_inc(gate_step, 1)
                dve.wait_ge(gate_step, k + 4)
                dve.reciprocal(rdn[:, :], dn1[:, :]).then_inc(gate_step, 1)
                dve.wait_ge(gate_step, k + 5)
                dve.tensor_tensor(crdn[:, :], rdn[:, :], cfac[:, rows], ALU.mult).then_inc(gate_step, 1)
                dve.wait_ge(gate_exp, g + 1)
                dve.tensor_scalar(ez1[:, :, :], ez[:, :, :], 1.0, None, ALU.add).then_inc(gate_step, 1)
                dve.wait_ge(gate_step, k + 7)
                dve.reciprocal(gate[:, :, :], ez1[:, :, :]).then_inc(gate_step, 1)
                dve.wait_ge(gate_step, k + 8)
                dve.tensor_tensor(ca[:, :], crdn[:, :], gate[:, :, 0], ALU.mult).then_inc(gate_step, 1)

            def add_bias(g, ib):
                v = stage[:, ib, 1, 0:D]
                dve.tensor_tensor(v, v, bias_bc[:, 0:D], ALU.add).then_inc(ep_step, 1)

            def mix(g, ib, step):
                v, y = stage[:, ib, 1, 0:D], stage[:, ib, 0, 2:MC]
                dve.wait_ge(ep_step, step)
                if ib == 0:
                    dve.wait_ge(gate_step, g * 9 + 9)
                dve.tensor_scalar(v, v, gate[:, ib, 1:2], None, ALU.mult).then_inc(ep_step, 1)
                dve.wait_ge(ep_step, step + 1)
                dve.scalar_tensor_tensor(out=y, in0=y, scalar=ca[:, ib:ib + 1], in1=v,
                                         op0=ALU.mult, op1=ALU.add).then_inc(y_done, 1)

            for b in range(2):
                stat(b, b, 16)
            dve.wait_ge(a_in, 16)
            dve.wait_ge(w_in, 16)
            for c in range(KC):
                for i, sign in ((0, 1.0), (1, -1.0)):
                    if c or i:
                        dve.wait_ge(w_step, KC * c + i)
                    dve.tensor_tensor_reduce(out=wprod[:, :], in0=wraw[:, c, 0, 0:D], in1=a_bc[:, i, :], scale=sign,
                                             scalar=0.0, op0=ALU.mult, op1=ALU.add,
                                             accum_out=wraw[:, c, 0, D + i:D + i + 1]).then_inc(w_step, 1)
            dve.wait_ge(w_step, 4)
            dve.tensor_copy(w_hi[:, :, 0, D:WC], wraw[:, :, 0, D:WC]).then_inc(w_step, 1)
            dve.wait_ge(w_step, 5)
            dve.wait_ge(w_hi_done, 2)
            flat = "p c t n -> p (c t n)"
            dve.tensor_tensor(w_lo[:, :, :, :].rearrange(flat), wraw[:, :, :, :].rearrange(flat),
                              w_hi[:, :, :, :].bitcast(F32).rearrange(flat), ALU.subtract).then_inc(w_ready, 1)
            rest_x(0, 0)
            stat(2, 2, 16)
            stat(3, 3, 16)
            rest_x(1, 1)
            stat(4, 4, 16)
            stat(5, 5, 16)
            rest_x(2, 2)
            rest_feat(0, 0)
            stat(6, 6, 16)
            stat(7, 7, 16)
            with dve.Fori(0, TAIL // AB) as m:
                for c in range(1, AB + 1):
                    k = c + AB - 1
                    rest_x(m * AB + (c + 2), (c + 2) % AB)
                    stat(m * AB + k, k % AB, m * 16 + 16 * (k // AB + 1), last=scales_of(m, k - AB) if k - AB >= 4
                         else m * AB + 8)
                    rest_feat(m * AB + c, c % AB)
            feats = (feat_hi, feat_lo)
            dve.wait_ge(flo_done, TAIL)
            whole(lr, feats, 0, TAIL - 1, 0, MC).then_inc(lr_done, 1)
            for b in range(TAIL, NB):
                if b + 2 < NB:
                    rest_x(b + 2, (b + 2) % AB)
                if b == NB - 3:
                    dve.wait_ge(cap_done, 1)
                    to_g(0, 0, 0)
                if b == NB - 2:
                    unit(0, 1, 1)
                rest_feat(b, b % AB)
            dve.wait_ge(flo_done, NB)
            whole(lr, feats, TAIL - 1, NB, 0, MC).then_inc(lr_done, 1)
            unit(0, 2, 2)
            whole(own, feats, 0, NB, 1, MC + 2).then_inc(own_done, 1)
            dve.wait_ge(own_done, 1)
            dve.wait_ge(bias_in, 16)
            dve.tensor_tensor(own[:, :, :], own[:, :, :],
                              bias_bc[:, D:D + 2].rearrange("p (o c) -> p o c", o=1).to_broadcast((P, NB, 2)), ALU.add).then_inc(own_done, 1)
            dve.wait_ge(cap_done, 2)
            dve.wait_ge(own_done, 2)
            for j in range(3, LEAD):
                unit(0, j, j % RING)
            with dve.Fori(0, NG - 1) as g:
                with dve.Fori(0, (NB - 1 - LEAD) // 4) as m:
                    for c in range(4):
                        unit(g, m * 4 + (LEAD + c), (LEAD + c) % RING)
                unit(g, NB - 1, (NB - 1) % RING)
                for j in range(3):
                    unit(g + 1, j, j)
                small_steps(g)
                for j in range(3, LEAD):
                    unit(g + 1, j, j % RING)
                    if j % 2 == 1:
                        ib = (j - 3) // 2
                        add_bias(g, ib)
                        mix(g, ib, g * (2 * GB) + (2 * ib + 1))
            with dve.Fori(0, (NB - 1 - LEAD) // 4) as m:
                for c in range(4):
                    unit(NG - 1, m * 4 + (LEAD + c), (LEAD + c) % RING)
            unit(NG - 1, NB - 1, (NB - 1) % RING)
            to_lo(NG * NB - 1, RING - 1)
            for ib in range(GB):
                dve.wait_ge(acc_free, (NG - 1) * GB + ib + 1)
                add_bias(NG - 1, ib)
            small_steps(NG - 1)
            for ib in range(GB):
                mix(NG - 1, ib, (NG - 1) * 2 * GB + GB + ib)

        @block.tensor
        def _(pe):
            def turn(b, s):
                pe.wait_ge(xn_done, b + 1)
                if not (isinstance(b, int) and b < 2):
                    pe.wait_ge(xlo_done, b - 1)
                for c in range(KC):
                    mm = pe.transpose(pt[:, s % 2, c * P:(c + 1) * P], xn[:, s % 2, c * P:(c + 1) * P], ident[:, :])
                mm.then_inc(xt_done, 1)

            def features(b, s):
                pe.wait_ge(xlo_done, b + 1)
                if not (isinstance(b, int) and b < 2):
                    pe.wait_ge(flo_done, b - 1)
                for t in range(2):
                    parts = [(xa, wa, c) for c in range(KC) for xa, wa in ((xt_hi, w_hi), (xt_hi, w_lo), (xt_lo, w_hi))]
                    for i, (xa, wa, c) in enumerate(parts):
                        mm = pe.matmul(pf[:, s % 2, t, 0:WC], xa[:, s % XS, c, :], wa[:, c, t, :],
                                       start=(i == 0), stop=(i == len(parts) - 1))
                mm.then_inc(feat_done, 1)

            def unit(g, j, s, free=None, last=False):
                n = g * NB + j
                first = free is not None
                pe.wait_ge(mask_done, n + 1)
                pe.wait_ge(glo_done, n + 1)

                def feat(f, t, c0, c1):
                    return f[:, bass.ds(j, 1), t, c0:c1].rearrange("p b n -> p (b n)")
                for ib in range(GB):
                    cols = slice(ib * P, (ib + 1) * P)
                    if first:
                        free(ib)
                    for i, f in enumerate((feat_hi, feat_lo)):
                        mm = pe.matmul(acc[:, ib, 1, 0:MC], mask[:, s, cols], feat(f, 1, 2, 2 + MC),
                                       start=(first and i == 0), stop=(last and i == 1))
                    pe.matmul(acc[:, ib, 0, 0:MC], g_hi[:, s, cols], feat(feat_hi, 0, 0, MC), start=first, stop=False)
                    pe.matmul(acc[:, ib, 0, 2:MC], g_hi[:, s, cols], feat(feat_lo, 0, 2, MC), start=False, stop=False)
                    mm = pe.matmul(acc[:, ib, 0, 0:MC], g_lo[:, s, cols], feat(feat_hi, 0, 0, MC), start=False, stop=last)
                    if last and ib < GB - 1:
                        mm.then_inc(acc_done, 1)
                mm.then_inc(mm_done, 1)

            pe.wait_ge(const_done, 3)
            turn(0, 0)
            turn(1, 1)
            turn(2, 2)
            pe.wait_ge(w_ready, 1)
            features(0, 0)
            turn(3, 3)
            features(1, 1)
            with pe.Fori(0, TAIL // AB) as m:
                for c in range(2, AB + 2):
                    turn(m * AB + (c + 2), (c + 2) % AB)
                    features(m * AB + c, c % AB)
            for b in range(TAIL + 1, NB):
                if b + 2 < NB:
                    turn(b + 2, (b + 2) % AB)
                features(b, b % AB)

            pe.wait_ge(ones_set, 2)

            def free_of_features(ib):
                if ib in (1, 2):
                    pe.wait_ge(flo_done, NB - 2 + ib)

            unit(0, 0, 0, free=free_of_features)
            def units(g):
                with pe.Fori(0, (NB - 4) // 4) as m:
                    for c in range(1, 5):
                        unit(g, m * 4 + c, c % RING)
                for j in range(NB - 3, NB):
                    unit(g, j, j % RING, last=(j == NB - 1))

            with pe.Fori(0, NG - 1) as g:
                units(g)
                unit(g + 1, 0, 0, free=lambda ib: pe.wait_ge(acc_free, g * GB + (ib + 1)))
            units(NG - 1)


def kernel(x, adj, L0_gnn_W_sa, L0_gnn_a_sa, L0_gnn_W_gcnb, L0_gnn_b_gcnb, L0_gnn_Wa, L0_gnn_ba, L0_gnn_Wb, L0_gnn_bb):
    import concourse.bacc as _bacc
    from concourse.bass_utils import run_bass_kernel_spmd as _run

    x = np.asarray(x)
    n, d = x.shape
    kc = d // P
    adjt = np.asarray(adj).reshape(n // GW, GW, n // P, P).transpose(0, 2, 3, 1).reshape(-1, P, GW)
    w = np.zeros((kc, P, 2, d + 4), x.dtype)
    w[:, :, 0, 0:d] = np.asarray(L0_gnn_W_sa).reshape(kc, P, d)
    w[:, :, 1, 0:d] = np.asarray(L0_gnn_W_gcnb).reshape(kc, P, d)
    for col, gate in ((0, L0_gnn_Wa), (1, L0_gnn_Wb)):
        top, bottom = np.asarray(gate).reshape(2, kc, P)
        w[:, :, 1, d + col], w[:, :, 1, d + 2 + col] = top, bottom
    w = w.transpose(1, 0, 2, 3).reshape(P, -1)
    biases = np.concatenate([np.asarray(L0_gnn_b_gcnb), np.asarray(L0_gnn_ba), np.asarray(L0_gnn_bb)]).reshape(1, -1)
    ins = {"x": x, "adjt": adjt, "weights": w, "a_sa": L0_gnn_a_sa, "biases": biases}

    nc = _bacc.Bacc("TRN2", target_bir_lowering=False, num_devices=1)
    arrays, args = {}, []
    for name, v in ins.items():
        a = np.ascontiguousarray(v)
        arrays[f"in_{name}"] = a
        args.append(nc.dram_tensor(f"in_{name}", a.shape, mybir.dt.from_np(a.dtype), kind="ExternalInput").ap())
    args.append(nc.dram_tensor("out_0", (n, d), F32, kind="ExternalOutput").ap())
    build(nc, *args)
    r = _run(nc, [arrays], core_ids=[0])
    return r.results[0]["out_0"]
```

```python
from contextlib import ExitStack

import numpy as np

import concourse.bass as bass
from concourse import mybir

F32 = mybir.dt.float32
F32R = mybir.dt.float32r
ALU = mybir.AluOpType
ACT = mybir.ActivationFunctionType
AX_X = mybir.AxisListType.X

P = 128
GB = 4
GW = GB * P
SLOPE = 0.01
LN_EPS = 1e-5
DEN_EPS = 1e-5
Z_MIN = -88.0
RING = 4


def build(nc, x, adjt, weights, a_sa, biases, out):
    N, D = x.shape
    NB = N // P
    NG = N // GW
    KC = D // P
    WC = D + 4
    FC = 2 + WC
    MC = D + 2
    START = (0, 2)
    AB = 8
    XS = 4
    TAIL = 1 + (NB - 1) // AB * AB
    LEAD = 11
    PLEAD = 16
    assert NB % RING == 0 and NB >= PLEAD + RING and (NB - 1 - LEAD) % RING == 0 and D == 2 * P

    sl_dram = nc.dram_tensor("sl_scratch", [NB, P], F32, kind="Internal").ap()

    with ExitStack() as top:
        def sem(name):
            return top.enter_context(nc.semaphore(name))

        def sbuf(stack, name, shape, dt):
            return stack.enter_context(nc.sbuf_tensor(name, shape, dt))

        def psum(stack, name, shape, dt):
            return stack.enter_context(nc.psum_tensor(name, shape, dt))

        feat_hi = sbuf(top, "feat_hi", [P, NB, 2, FC], F32R)
        feat_lo = sbuf(top, "feat_lo", [P, NB, 2, FC], F32R)
        raw = sbuf(top, "raw", [P, RING, GW], F32)
        mask = sbuf(top, "mask", [P, RING, GW], F32R)
        e = sbuf(top, "e", [P, RING, GW], F32)
        g_hi = sbuf(top, "g_hi", [P, RING, GW], F32R)
        g_lo = sbuf(top, "g_lo", [P, RING, GW], F32R)
        lr = sbuf(top, "lr", [P, NB, 2], F32)
        own = sbuf(top, "own", [P, NB, 2], F32)
        cap = sbuf(top, "cap", [P, NB], F32)
        cfac = sbuf(top, "cfac", [P, NB], F32)
        bias_bc = sbuf(top, "bias_bc", [P, D + 2], F32)

        pa = ExitStack()
        xin = sbuf(pa, "xin", [P, AB, D], F32)
        xn = sbuf(pa, "xn", [P, 2, D], F32)
        ident = sbuf(pa, "ident", [P, P], F32)
        wprod = sbuf(pa, "wprod", [P, D], F32)
        wraw = sbuf(pa, "wraw", [P, KC, 2, WC], F32)
        w_hi = sbuf(pa, "w_hi", [P, KC, 2, WC], F32R)
        w_lo = sbuf(pa, "w_lo", [P, KC, 2, WC], F32R)
        xt_hi = sbuf(pa, "xt_hi", [P, XS, KC, P], F32R)
        xt_lo = sbuf(pa, "xt_lo", [P, XS, KC, P], F32R)
        a_bc = sbuf(pa, "a_bc", [P, 2, D], F32)
        stats = sbuf(pa, "stats", [P, AB, 6], F32)
        mv = sbuf(pa, "mv", [P, AB, 2], F32)
        half = sbuf(pa, "half", [P, 2], F32)
        warm = sbuf(pa, "warm", [P, 1], F32)
        veps = sbuf(pa, "veps", [P, AB], F32)
        rstd = sbuf(pa, "rstd", [P, AB], F32)
        mr = sbuf(pa, "mr", [P, AB], F32)
        nmr = sbuf(pa, "nmr", [P, AB], F32)
        pt = psum(pa, "pt", [P, 2, 512], F32)
        pf = psum(pa, "pf", [P, 2, 2, 512], F32)
        pa.close()

        stage = sbuf(top, "stage", [P, GB, 2, FC], F32)
        xres = sbuf(top, "xres", [P, GB, D], F32)
        lbc = sbuf(top, "lbc", [P, NG, GW], F32)
        z = sbuf(top, "z", [P, GB, 2], F32)
        zc = sbuf(top, "zc", [P, GB, 2], F32)
        ez = sbuf(top, "ez", [P, GB, 2], F32)
        ez1 = sbuf(top, "ez1", [P, GB, 2], F32)
        gate = sbuf(top, "gate", [P, GB, 2], F32)
        dn = sbuf(top, "dn", [P, GB], F32)
        dn1 = sbuf(top, "dn1", [P, GB], F32)
        rdn = sbuf(top, "rdn", [P, GB], F32)
        crdn = sbuf(top, "crdn", [P, GB], F32)
        ca = sbuf(top, "ca", [P, GB], F32)
        acc = psum(top, "acc", [P, GB, 2, 512], F32)

        w_in = sem("w_in")
        a_in = sem("a_in")
        bias_in = sem("bias_in")
        x_in = [sem(f"x_in{i}") for i in range(AB // 2)]
        const_done = sem("const_done")
        ones_set = sem("ones_set")
        warm_done = sem("warm_done")
        w_step = sem("w_step")
        w_hi_done = sem("w_hi_done")
        w_ready = sem("w_ready")
        stat_done = sem("stat_done")
        mv_done = sem("mv_done")
        pow_step = sem("pow_step")
        xn_done = sem("xn_done")
        xt_done = sem("xt_done")
        xhi_done = sem("xhi_done")
        xlo_done = sem("xlo_done")
        feat_done = sem("feat_done")
        bank_done = sem("bank_done")
        fhi_done = sem("fhi_done")
        flo_done = sem("flo_done")
        lr_done = sem("lr_done")
        own_done = sem("own_done")
        cap_done = sem("cap_done")
        cfac_done = sem("cfac_done")
        l_stored = sem("l_stored")
        l_stored_rest = sem("l_stored_rest")
        l_in = sem("l_in")
        adj_in = [sem("adj_in0"), sem("adj_in1")]
        mask_done = sem("mask_done")
        exp_done = sem("exp_done")
        g_done = sem("g_done")
        ghi_done = sem("ghi_done")
        glo_done = sem("glo_done")
        mm_done = sem("mm_done")
        acc_done = sem("acc_done")
        acc_free = sem("acc_free")
        gate_step = sem("gate_step")
        gate_exp = sem("gate_exp")
        ep_step = sem("ep_step")
        conv_scaled = sem("conv_scaled")
        y_done = sem("y_done")
        tanh_done = sem("tanh_done")
        sig_done = sem("sig_done")
        fin_done = sem("fin_done")
        sig_dve = sem("sig_dve")
        fin_dve = sem("fin_dve")
        res_in = sem("res_in")
        out_done = sem("out_done")
        passed = {nc.scalar.engine: sem("act_passed"), nc.vector.engine: sem("dve_passed"), nc.gpsimd.engine: sem("pool_passed")}

        def apart(eng):
            eng.sem_inc(passed[eng.engine], 1)

        def scales_of(m, k):
            return m * (2 * AB) + 4 * (k // 2 + 1)

        block = top.enter_context(nc.Block())

        xb = x.rearrange("(b p) d -> p b d", p=P)
        ob = out.rearrange("(b p) d -> p b d", p=P)

        @block.sync
        def _(sp):
            def load_x(b, s):
                sp.dma_start(xin[:, s:s + 2, :], xb[:, bass.ds(b, 2), :]).then_inc(x_in[s // 2], 16)

            def load_adj(q, s):
                sp.dma_start(raw[:, s:s + 2, :].rearrange("p s i -> p (s i)"), adjt[bass.ds(q, 1), :, :]
                             .rearrange("q p f -> p (q f)")).then_inc(adj_in[s // 2], 16)

            load_x(0, 0)
            sp.dma_start(a_bc[:, :, :].rearrange("p c n -> p (c n)"), a_sa.to_broadcast((P, 2 * D))).then_inc(a_in, 16)
            for s in range(2, AB, 2):
                load_x(s, s)
            load_adj(0, 0)
            load_adj(1, 2)
            sp.dma_start(bias_bc[:, :], biases.to_broadcast((P, D + 2))).then_inc(bias_in, 16)
            with sp.Fori(1, NB // AB) as m:
                for s in range(0, AB, 2):
                    sp.wait_ge(xn_done, m * AB + (s + 2 - AB))
                    load_x(m * AB + s, s)

            def adj_body(k):
                for s in (0, 2):
                    sp.wait_ge(mask_done, k * RING + (s - 2))
                    load_adj(k * 2 + s // 2, s)

            NK = NB // RING
            adj_body(1)
            l_flat = sl_dram.rearrange("(o b) p -> o (b p)", o=1)
            l_col = sl_dram.rearrange("b p -> p b")
            lbc_f = lbc[:, :, :].rearrange("p g i -> p (g i)")
            with nc.allow_non_contiguous_dma(reason="a column of l a block: 16 KB in all"):
                sp.wait_ge(lr_done, 1)
                sp.dma_start(l_col[:, 0:GB], lr[:, 0:GB, 0]).then_inc(l_stored, 16)
                sp.wait_ge(l_stored, 16)
                sp.dma_start(lbc_f[:, 0:GW], l_flat[:, 0:GW].to_broadcast((P, GW))).then_inc(l_in, 16)
                sp.wait_ge(lr_done, 2)
                sp.dma_start(l_col[:, GB:NB], lr[:, GB:NB, 0]).then_inc(l_stored_rest, 16)

            sp.wait_ge(feat_done, NB)
            sp.dma_start(xres[:, :, :], xb[:, 0:GB, :]).then_inc(res_in, 16)
            with sp.Fori(2, NK) as m:
                adj_body(m)
            sp.wait_ge(l_stored_rest, 16)
            with sp.Fori(0, NG - 1) as g:
                sp.dma_start(lbc_f[:, bass.ds(g * GW + GW, GW)],
                             l_flat[:, bass.ds(g * GW + GW, GW)].to_broadcast((P, GW))).then_inc(l_in, 16)
                for k in range(PLEAD // RING + 1):
                    adj_body(g * NK + (NK + k))
                sp.wait_ge(fin_done, g + 2)
                sp.dma_start(ob[:, bass.ds(g * GB, GB), :], xres[:, :, :]).then_inc(out_done, 16)
                sp.wait_ge(out_done, g * 16 + 16)
                sp.dma_start(xres[:, :, :], xb[:, bass.ds(g * GB + GB, GB), :]).then_inc(res_in, 16)
                with sp.Fori(PLEAD // RING + 1, NK) as m:
                    adj_body(g * NK + m + NK)
            for ib in range(GB):
                if ib < GB // 2:
                    sp.wait_ge(fin_done, NG + 1 + ib)
                else:
                    sp.wait_ge(fin_dve, ib + 1 - GB // 2)
                sp.dma_start(ob[:, (NG - 1) * GB + ib, :], xres[:, ib, :]).then_inc(out_done, 16)
            sp.wait_ge(out_done, (NG - 1 + GB) * 16)

        @block.gpsimd
        def _(pool):
            pool.memset(half[:, :], -0.5).then_inc(const_done, 1)
            pool.memset(ident[:, :], 0.0).then_inc(const_done, 1)
            pool.wait_ge(const_done, 2)
            pool.affine_select(out=ident[:, :], in_=ident[:, :], compare_op=ALU.not_equal, fill=1.0,
                               base=0, pattern=[[-1, P]], channel_multiplier=1).then_inc(const_done, 1)
            pool.sem_inc(fin_done, 1)

            def to_mask(n, s, first=False):
                if s % 2 == 0:
                    pool.wait_ge(adj_in[s // 2], n * 4 + (16 - 4 * s))
                if not first:
                    pool.wait_ge(mm_done, n - (RING - 1))
                apart(pool)
                pool.tensor_scalar(mask[:, s, :], raw[:, s, :], 1.0, 0.0, ALU.mult, ALU.add).then_inc(mask_done, 1)

            def to_rstd(b, s, steps):
                pool.wait_ge(mv_done, b + 2)
                if not isinstance(b, int):
                    pool.wait_ge(xn_done, b + (2 - AB))
                apart(pool)
                r = slice(s, s + 2)
                pool.tensor_scalar(veps[:, r], mv[:, r, 1], LN_EPS, None, ALU.add).then_inc(pow_step, 1)
                pool.wait_ge(pow_step, steps + 1)
                pool.tensor_tensor(rstd[:, r], veps[:, r], half[:, :], ALU.pow).then_inc(pow_step, 1)
                pool.wait_ge(pow_step, steps + 2)
                pool.tensor_tensor(mr[:, r], mv[:, r, 0], rstd[:, r], ALU.mult).then_inc(pow_step, 1)
                pool.wait_ge(pow_step, steps + 3)
                apart(pool)
                pool.tensor_scalar(nmr[:, r], mr[:, r], -1.0, None, ALU.mult).then_inc(pow_step, 1)

            to_rstd(0, 0, 0)
            pool.memset(feat_hi[:, :, 0, 0:1].bitcast(F32), 1.0).then_inc(ones_set, 1)
            pool.memset(feat_hi[:, :, 0, 1:2].bitcast(F32), 0.0).then_inc(ones_set, 1)
            for b in range(2, AB, 2):
                to_rstd(b, b, 2 * b)
                if b >= RING:
                    for n in (b - RING, b - RING + 1):
                        to_mask(n, n, True)
            with pool.Fori(1, NB // AB) as m:
                for s in range(0, AB, 2):
                    to_rstd(m * AB + s, s, m * (2 * AB) + 2 * s)

            with pool.Fori(1, PLEAD // 4) as m:
                for s in range(4):
                    to_mask(m * 4 + s, s)

            def finish(g, ibs, k):
                pool.wait_ge(tanh_done, g + (k + 1))
                t = stage[:, ibs, 0, 2:MC]
                apart(pool)
                pool.tensor_scalar(t, t, 0.5, 0.5, ALU.mult, ALU.add).then_inc(sig_done, 1)
                pool.wait_ge(sig_done, g + (k + 1))
                if k == 0:
                    pool.wait_ge(res_in, g * 16 + 16)
                pool.tensor_tensor(xres[:, ibs, :], t, xres[:, ibs, :], ALU.add).then_inc(fin_done, 1)

            with pool.Fori(0, NG - 1) as g:
                with pool.Fori(PLEAD // 4, NB // 4 + PLEAD // 4) as m:
                    for s in range(4):
                        to_mask(g * NB + m * 4 + s, s)
                finish(g, slice(0, GB), 0)
            with pool.Fori(PLEAD // 4, NB // 4) as m:
                for s in range(4):
                    to_mask(m * 4 + ((NG - 1) * NB + s), s)
            for ib in range(GB // 2):
                finish(NG - 1, ib, ib)

        @block.scalar
        def _(act):
            act.dma_start(wraw[:, :, :, :].rearrange("p c t n -> p (c t n)"), weights).then_inc(w_in, 16)

            act.wait_ge(const_done, 1)
            act.activation(warm[:, :], half[:, 0:1], ACT.Exp).then_inc(warm_done, 1)

            def norm(b, s, scales):
                act.wait_ge(pow_step, scales)
                if not (isinstance(b, int) and b < 2):
                    act.wait_ge(xt_done, b - 1)
                apart(act)
                act.activation(xn[:, s % 2, :], xin[:, s, :], ACT.Identity, bias=nmr[:, s:s + 1],
                               scale=rstd[:, s:s + 1]).then_inc(xn_done, 1)

            def split_x(b, s):
                act.wait_ge(xt_done, b + 1)
                if not (isinstance(b, int) and b < XS):
                    act.wait_ge(feat_done, b - (XS - 1))
                act.activation(xt_hi[:, s % XS, :, :], pt[:, s % 2, 0:D].rearrange("p (c n) -> p c n", c=KC),
                               ACT.Relu).then_inc(xhi_done, 1)

            def split_feat(b, s):
                for t in range(2):
                    act.wait_ge(bank_done if t == 0 else feat_done, b + 1)
                    apart(act)
                    act.activation(feat_hi[:, bass.ds(b, 1), t, 2:FC].rearrange("p b n -> p (b n)"),
                                   pf[:, s % 2, t, 0:WC], ACT.Copy).then_inc(fhi_done, 1)

            def to_exp(n, g, j, s, first=False):
                if not first:
                    act.wait_ge(glo_done, n - (RING - 1))
                apart(act)
                act.activation(e[:, s, :], lbc[:, bass.ds(g, 1), :].rearrange("p g i -> p (g i)"), ACT.Exp,
                               bias=lr[:, bass.ds(j, 1), 1], scale=-(1.0 - SLOPE)).then_inc(exp_done, 1)

            def to_hi(n, s, first=False):
                act.wait_ge(g_done, n + 1)
                if not first:
                    act.wait_ge(mm_done, n - (RING - 1))
                act.activation(g_hi[:, s, :], e[:, s, :], ACT.Copy).then_inc(ghi_done, 1)

            def unit(g, j, s):
                n = g * NB + j
                to_exp(n, g, j, s, first=isinstance(n, int) and n < RING)
                to_hi(n - 1, (s - 1) % RING, first=isinstance(n, int) and n - 1 < RING)

            def move_sums(g):
                act.wait_ge(fin_done, g + 1)
                for ib in range(GB):
                    if ib < GB - 1:
                        act.wait_ge(acc_done, g * (GB - 1) + (ib + 1))
                    else:
                        act.wait_ge(mm_done, g * NB + NB)
                    act.activation(stage[:, ib, :, 0:MC], acc[:, ib, :, 0:MC], ACT.Copy).then_inc(acc_free, 1)
                act.wait_ge(gate_step, g * 9 + 3)
                act.activation(ez[:, :, :], zc[:, :, :], ACT.Exp, scale=-1.0).then_inc(gate_exp, 1)

            def last_sigmoid(g, ibs, k):
                act.wait_ge(y_done, g * GB + (k + 1 if ibs == k else GB))
                t = stage[:, ibs, 0, 2:MC]
                act.activation(t, t, ACT.Tanh, scale=0.5).then_inc(tanh_done, 1)

            for b in range(3):
                norm(b, b, scales_of(0, b))
                if b:
                    split_x(b - 1, b - 1)
                if b == 0:
                    act.wait_ge(w_in, 16)
                    act.activation(w_hi[:, :, 0, 0:D], wraw[:, :, 0, 0:D], ACT.Copy).then_inc(w_hi_done, 1)
                    act.activation(w_hi[:, :, 1, :], wraw[:, :, 1, :], ACT.Copy).then_inc(w_hi_done, 1)
            norm(3, 3, scales_of(0, 3))
            split_x(2, 2)
            split_feat(0, 0)
            norm(4, 4, scales_of(0, 4))
            split_x(3, 3)
            split_feat(1, 1)
            with act.Fori(0, TAIL // AB) as m:
                for c in range(2, AB + 2):
                    norm(m * AB + (c + 3), (c + 3) % AB, scales_of(m, c + 3))
                    split_x(m * AB + (c + 2), (c + 2) % AB)
                    split_feat(m * AB + c, c % AB)
            for b in range(TAIL + 1, NB):
                if b + 3 < NB:
                    norm(b + 3, (b + 3) % AB, scales_of(0, b + 3))
                if b + 2 < NB:
                    split_x(b + 2, (b + 2) % AB)
                if b == TAIL + 1:
                    act.wait_ge(lr_done, 1)
                    act.activation(cap[:, 0:TAIL - 1], lr[:, 0:TAIL - 1, 1], ACT.Exp, scale=SLOPE).then_inc(cap_done, 1)
                if b == NB - 3:
                    act.wait_ge(l_in, 16)
                    to_exp(0, 0, 0, 0, first=True)
                if b == NB - 2:
                    unit(0, 1, 1)
                split_feat(b, b % AB)
            unit(0, 2, 2)
            act.wait_ge(lr_done, 2)
            act.activation(cap[:, TAIL - 1:NB], lr[:, TAIL - 1:NB, 1], ACT.Exp, scale=SLOPE).then_inc(cap_done, 1)
            act.activation(cfac[:, :], lr[:, :, 0], ACT.Exp, scale=-SLOPE).then_inc(cfac_done, 1)
            for j in range(3, LEAD):
                unit(0, j, j % RING)
            with act.Fori(0, NG - 1) as g:
                with act.Fori(0, (NB - 1 - LEAD) // 4) as m:
                    for c in range(4):
                        unit(g, m * 4 + (LEAD + c), (LEAD + c) % RING)
                unit(g, NB - 1, (NB - 1) % RING)
                act.wait_ge(l_in, g * 16 + 32)
                for j in range(3):
                    unit(g + 1, j, j)
                move_sums(g)
                for j in range(3, LEAD):
                    unit(g + 1, j, j % RING)
                last_sigmoid(g, slice(0, GB), 0)
            with act.Fori(0, (NB - 1 - LEAD) // 4) as m:
                for c in range(4):
                    unit(NG - 1, m * 4 + (LEAD + c), (LEAD + c) % RING)
            unit(NG - 1, NB - 1, (NB - 1) % RING)
            to_hi(NG * NB - 1, RING - 1)
            move_sums(NG - 1)
            act.wait_ge(gate_step, (NG - 1) * 9 + 8)
            for ib in range(GB):
                act.wait_ge(ep_step, (NG - 1) * 2 * GB + ib + 1)
                v = stage[:, ib, 1, 0:D]
                act.activation(v, v, ACT.Copy, scale=gate[:, ib, 1:2]).then_inc(conv_scaled, 1)
            for ib in range(GB):
                last_sigmoid(NG - 1, ib, ib)

        @block.vector
        def _(dve):
            def stat(b, s, arrived, last=None):
                if s % 2 == 0:
                    dve.wait_ge(x_in[s // 2], arrived)
                if last is not None:
                    dve.wait_ge(pow_step, last)
                dve.bn_stats(stats[:, s, :], xin[:, s, :]).then_inc(stat_done, 1)

            def aggregate(b, s):
                dve.wait_ge(stat_done, b + 1)
                apart(dve)
                dve.bn_aggr(mv[:, s, :], stats[:, s, :]).then_inc(mv_done, 1)

            def rest_x(b, s):
                dve.wait_ge(xhi_done, b + 1)
                dve.scalar_tensor_tensor(
                    out=xt_lo[:, s % XS, :, :].rearrange("p c n -> p (c n)"), in0=pt[:, s % 2, 0:D], scalar=0.0,
                    in1=xt_hi[:, s % XS, :, :].bitcast(F32).rearrange("p c n -> p (c n)"),
                    op0=ALU.max, op1=ALU.subtract).then_inc(xlo_done, 1)

            def rest_feat(b, s):
                for t in range(2):
                    dve.wait_ge(fhi_done, b * 2 + (t + 1))
                    dve.tensor_tensor(feat_lo[:, bass.ds(b, 1), t, 2:FC].rearrange("p b n -> p (b n)"),
                                      pf[:, s % 2, t, 0:WC],
                                      feat_hi[:, bass.ds(b, 1), t, 2:FC].bitcast(F32).rearrange("p b n -> p (b n)"),
                                      ALU.subtract).then_inc(flo_done, 1)

            def whole(out, f, b0, b1, t, c):
                return dve.tensor_tensor(out[:, b0:b1, :], f[0][:, b0:b1, t, c:c + 2].bitcast(F32),
                                         f[1][:, b0:b1, t, c:c + 2].bitcast(F32), ALU.add)

            def to_g(n, j, s):
                dve.wait_ge(exp_done, n + 1)
                dve.wait_ge(mask_done, n + 1)
                dve.scalar_tensor_tensor(out=e[:, s, :], in0=e[:, s, :], scalar=cap[:, bass.ds(j, 1)],
                                         in1=mask[:, s, :].bitcast(F32), op0=ALU.min, op1=ALU.mult).then_inc(g_done, 1)

            def to_lo(n, s):
                dve.wait_ge(ghi_done, n + 1)
                dve.tensor_tensor(g_lo[:, s, :], e[:, s, :], g_hi[:, s, :].bitcast(F32), ALU.subtract).then_inc(glo_done, 1)

            def unit(g, j, s):
                n = g * NB + j
                to_g(n, j, s)
                to_lo(n - 1, (s - 1) % RING)

            def small_steps(g):
                k = g * 9
                dve.wait_ge(acc_free, g * GB + GB)
                rows = bass.ds(g * GB, GB)
                dve.tensor_tensor(z[:, :, :], stage[:, :, 1, D:D + 2], own[:, rows, :], ALU.add).then_inc(gate_step, 1)
                dve.tensor_tensor(dn[:, :], stage[:, :, 0, 0], cfac[:, rows], ALU.mult).then_inc(gate_step, 1)
                dve.wait_ge(gate_step, k + 1)
                dve.tensor_scalar(zc[:, :, :], z[:, :, :], Z_MIN, None, ALU.max).then_inc(gate_step, 1)
                dve.wait_ge(gate_step, k + 2)
                dve.tensor_scalar(dn1[:, :], dn[:, :], DEN_EPS, None, ALU.add).then_inc(gate_step, 1)
                dve.wait_ge(gate_step, k + 4)
                dve.reciprocal(rdn[:, :], dn1[:, :]).then_inc(gate_step, 1)
                dve.wait_ge(gate_exp, g + 1)
                dve.tensor_scalar(ez1[:, :, :], ez[:, :, :], 1.0, None, ALU.add).then_inc(gate_step, 1)
                dve.wait_ge(gate_step, k + 5)
                dve.tensor_tensor(crdn[:, :], rdn[:, :], cfac[:, rows], ALU.mult).then_inc(gate_step, 1)
                dve.wait_ge(gate_step, k + 6)
                dve.reciprocal(gate[:, :, :], ez1[:, :, :]).then_inc(gate_step, 1)
                dve.wait_ge(gate_step, k + 8)
                dve.tensor_tensor(ca[:, :], crdn[:, :], gate[:, :, 0], ALU.mult).then_inc(gate_step, 1)

            def add_bias(g, ib):
                v = stage[:, ib, 1, 0:D]
                dve.tensor_tensor(v, v, bias_bc[:, 0:D], ALU.add).then_inc(ep_step, 1)

            def mix(g, ib, step):
                v, y = stage[:, ib, 1, 0:D], stage[:, ib, 0, 2:MC]
                if ib == 0:
                    dve.wait_ge(gate_step, g * 9 + 9)
                if step is None:
                    dve.wait_ge(conv_scaled, ib + 1)
                else:
                    dve.wait_ge(ep_step, step)
                    dve.tensor_scalar(v, v, gate[:, ib, 1:2], None, ALU.mult).then_inc(ep_step, 1)
                    dve.wait_ge(ep_step, step + 1)
                dve.scalar_tensor_tensor(out=y, in0=y, scalar=ca[:, ib:ib + 1], in1=v,
                                         op0=ALU.mult, op1=ALU.add).then_inc(y_done, 1)

            def rest_w(t):
                dve.tensor_tensor(w_lo[:, :, t, :], wraw[:, :, t, :], w_hi[:, :, t, :].bitcast(F32),
                                  ALU.subtract).then_inc(w_ready, 1)

            for b in (0, 1):
                stat(b, b, 16)
            for b in (0, 1):
                aggregate(b, b)
            dve.wait_ge(a_in, 16)
            dve.wait_ge(w_in, 16)
            for c in range(KC):
                for i, sign in ((0, 1.0), (1, -1.0)):
                    if c or i:
                        dve.wait_ge(w_step, KC * c + i)
                    dve.tensor_tensor_reduce(out=wprod[:, :], in0=wraw[:, c, 0, 0:D], in1=a_bc[:, i, :], scale=sign,
                                             scalar=0.0, op0=ALU.mult, op1=ALU.add,
                                             accum_out=wraw[:, c, 0, D + i:D + i + 1]).then_inc(w_step, 1)
            dve.wait_ge(w_step, 4)
            dve.tensor_copy(w_hi[:, :, 0, D:WC], wraw[:, :, 0, D:WC]).then_inc(w_step, 1)
            for b in (2, 3):
                stat(b, b, 16)
            for b in (2, 3):
                aggregate(b, b)
            dve.wait_ge(w_step, 5)
            dve.wait_ge(w_hi_done, 2)
            rest_w(0)
            rest_x(0, 0)
            rest_w(1)
            rest_x(1, 1)
            for b in (4, 5):
                stat(b, b, 16)
            for b in (4, 5):
                aggregate(b, b)
            rest_x(2, 2)
            rest_feat(0, 0)
            for b in (6, 7):
                stat(b, b, 16)
            for b in (6, 7):
                aggregate(b, b)
            with dve.Fori(0, TAIL // AB) as m:
                for c in range(1, AB + 1):
                    k = c + AB - 1
                    rest_x(m * AB + (c + 2), (c + 2) % AB)
                    stat(m * AB + k, k % AB, m * 16 + 16 * (k // AB + 1), last=scales_of(m, k - AB))
                    rest_feat(m * AB + c, c % AB)
                    aggregate(m * AB + k, k % AB)
            feats = (feat_hi, feat_lo)
            dve.wait_ge(flo_done, 2 * TAIL)
            whole(lr, feats, 0, TAIL - 1, 0, MC).then_inc(lr_done, 1)
            for b in range(TAIL, NB):
                if b + 2 < NB:
                    rest_x(b + 2, (b + 2) % AB)
                if b == NB - 3:
                    dve.wait_ge(cap_done, 1)
                    to_g(0, 0, 0)
                if b == NB - 2:
                    unit(0, 1, 1)
                rest_feat(b, b % AB)
            dve.wait_ge(flo_done, 2 * NB)
            whole(lr, feats, TAIL - 1, NB, 0, MC).then_inc(lr_done, 1)
            unit(0, 2, 2)
            dve.wait_ge(cap_done, 2)
            for j in range(3, LEAD):
                unit(0, j, j % RING)
            whole(own, feats, 0, NB, 1, MC + 2).then_inc(own_done, 1)
            dve.wait_ge(own_done, 1)
            dve.wait_ge(bias_in, 16)
            dve.tensor_tensor(own[:, :, :], own[:, :, :],
                              bias_bc[:, D:D + 2].rearrange("p (o c) -> p o c", o=1).to_broadcast((P, NB, 2)), ALU.add).then_inc(own_done, 1)
            dve.wait_ge(own_done, 2)
            with dve.Fori(0, NG - 1) as g:
                with dve.Fori(0, (NB - 1 - LEAD) // 4) as m:
                    for c in range(4):
                        unit(g, m * 4 + (LEAD + c), (LEAD + c) % RING)
                unit(g, NB - 1, (NB - 1) % RING)
                for j in range(3):
                    unit(g + 1, j, j)
                small_steps(g)
                for j in range(3, LEAD):
                    unit(g + 1, j, j % RING)
                    if j % 2 == 1:
                        ib = (j - 3) // 2
                        add_bias(g, ib)
                        mix(g, ib, g * (2 * GB) + (2 * ib + 1))
            with dve.Fori(0, (NB - 1 - LEAD) // 4) as m:
                for c in range(4):
                    unit(NG - 1, m * 4 + (LEAD + c), (LEAD + c) % RING)
            unit(NG - 1, NB - 1, (NB - 1) % RING)
            to_lo(NG * NB - 1, RING - 1)
            for ib in range(GB - 1):
                dve.wait_ge(acc_free, (NG - 1) * GB + ib + 1)
                add_bias(NG - 1, ib)
            small_steps(NG - 1)
            add_bias(NG - 1, GB - 1)
            for ib in range(GB):
                mix(NG - 1, ib, None)
            for k, ib in enumerate(range(GB // 2, GB)):
                dve.wait_ge(tanh_done, NG + ib)
                t = stage[:, ib, 0, 2:MC]
                dve.tensor_scalar(t, t, 0.5, 0.5, ALU.mult, ALU.add).then_inc(sig_dve, 1)
                dve.wait_ge(sig_dve, k + 1)
                dve.wait_ge(res_in, NG * 16)
                dve.tensor_tensor(xres[:, ib, :], t, xres[:, ib, :], ALU.add).then_inc(fin_dve, 1)

        @block.tensor
        def _(pe):
            def turn(b, s):
                pe.wait_ge(xn_done, b + 1)
                if not (isinstance(b, int) and b < 2):
                    pe.wait_ge(xlo_done, b - 1)
                for c in range(KC):
                    mm = pe.transpose(pt[:, s % 2, c * P:(c + 1) * P], xn[:, s % 2, c * P:(c + 1) * P], ident[:, :])
                mm.then_inc(xt_done, 1)

            def features(b, s):
                pe.wait_ge(xlo_done, b + 1)
                for t in range(2):
                    if isinstance(b, int) and b == 0:
                        pe.wait_ge(w_ready, t + 1)
                    if not (isinstance(b, int) and b < 2):
                        pe.wait_ge(flo_done, b * 2 + (t - 3))
                    parts = [(xa, wa, c) for c in range(KC) for xa, wa in ((xt_hi, w_hi), (xt_hi, w_lo), (xt_lo, w_hi))]
                    for i, (xa, wa, c) in enumerate(parts):
                        mm = pe.matmul(pf[:, s % 2, t, 0:WC], xa[:, s % XS, c, :], wa[:, c, t, :],
                                       start=(i == 0), stop=(i == len(parts) - 1))
                    mm.then_inc(feat_done if t else bank_done, 1)

            def unit(g, j, s, free=None, last=False):
                n = g * NB + j
                first = free is not None
                pe.wait_ge(mask_done, n + 1)
                pe.wait_ge(glo_done, n + 1)

                def feat(f, t, c0, c1):
                    return f[:, bass.ds(j, 1), t, c0:c1].rearrange("p b n -> p (b n)")
                for ib in range(GB):
                    cols = slice(ib * P, (ib + 1) * P)
                    if first:
                        free(ib)
                    for i, f in enumerate((feat_hi, feat_lo)):
                        mm = pe.matmul(acc[:, ib, 1, 0:MC], mask[:, s, cols], feat(f, 1, 2, 2 + MC),
                                       start=(first and i == 0), stop=(last and i == 1))
                    pe.matmul(acc[:, ib, 0, 0:MC], g_hi[:, s, cols], feat(feat_hi, 0, 0, MC), start=first, stop=False)
                    pe.matmul(acc[:, ib, 0, 2:MC], g_hi[:, s, cols], feat(feat_lo, 0, 2, MC), start=False, stop=False)
                    mm = pe.matmul(acc[:, ib, 0, 0:MC], g_lo[:, s, cols], feat(feat_hi, 0, 0, MC), start=False, stop=last)
                    if last and ib < GB - 1:
                        mm.then_inc(acc_done, 1)
                mm.then_inc(mm_done, 1)

            pe.wait_ge(const_done, 3)
            turn(0, 0)
            turn(1, 1)
            features(0, 0)
            turn(2, 2)
            features(1, 1)
            turn(3, 3)
            with pe.Fori(0, TAIL // AB) as m:
                for c in range(2, AB + 2):
                    turn(m * AB + (c + 2), (c + 2) % AB)
                    features(m * AB + c, c % AB)
            for b in range(TAIL + 1, NB):
                if b + 2 < NB:
                    turn(b + 2, (b + 2) % AB)
                features(b, b % AB)

            pe.wait_ge(ones_set, 2)

            def free_of_features(ib):
                if ib in (1, 2):
                    pe.wait_ge(flo_done, 2 * (NB - 2 + ib))

            unit(0, 0, 0, free=free_of_features)
            def units(g):
                with pe.Fori(0, (NB - 4) // 4) as m:
                    for c in range(1, 5):
                        unit(g, m * 4 + c, c % RING)
                for j in range(NB - 3, NB):
                    unit(g, j, j % RING, last=(j == NB - 1))

            with pe.Fori(0, NG - 1) as g:
                units(g)
                unit(g + 1, 0, 0, free=lambda ib: pe.wait_ge(acc_free, g * GB + (ib + 1)))
            units(NG - 1)


def kernel(x, adj, L0_gnn_W_sa, L0_gnn_a_sa, L0_gnn_W_gcnb, L0_gnn_b_gcnb, L0_gnn_Wa, L0_gnn_ba, L0_gnn_Wb, L0_gnn_bb):
    import concourse.bacc as _bacc
    from concourse.bass_utils import run_bass_kernel_spmd as _run

    x = np.asarray(x)
    n, d = x.shape
    kc = d // P
    adjt = np.asarray(adj).reshape(n // GW, GW, n // P // 2, 2, P).transpose(0, 2, 4, 3, 1).reshape(-1, P, 2 * GW)
    w = np.zeros((kc, P, 2, d + 4), x.dtype)
    w[:, :, 0, 0:d] = np.asarray(L0_gnn_W_sa).reshape(kc, P, d)
    w[:, :, 1, 0:d] = np.asarray(L0_gnn_W_gcnb).reshape(kc, P, d)
    for col, gate in ((0, L0_gnn_Wa), (1, L0_gnn_Wb)):
        top, bottom = np.asarray(gate).reshape(2, kc, P)
        w[:, :, 1, d + col], w[:, :, 1, d + 2 + col] = top, bottom
    w = w.transpose(1, 0, 2, 3).reshape(P, -1)
    biases = np.concatenate([np.asarray(L0_gnn_b_gcnb), np.asarray(L0_gnn_ba), np.asarray(L0_gnn_bb)]).reshape(1, -1)
    ins = {"x": x, "adjt": adjt, "weights": w, "a_sa": L0_gnn_a_sa, "biases": biases}

    nc = _bacc.Bacc("TRN2", target_bir_lowering=False, num_devices=1)
    arrays, args = {}, []
    for name, v in ins.items():
        a = np.ascontiguousarray(v)
        arrays[f"in_{name}"] = a
        args.append(nc.dram_tensor(f"in_{name}", a.shape, mybir.dt.from_np(a.dtype), kind="ExternalInput").ap())
    args.append(nc.dram_tensor("out_0", (n, d), F32, kind="ExternalOutput").ap())
    build(nc, *args)
    r = _run(nc, [arrays], core_ids=[0])
    return r.results[0]["out_0"]
```
